# Optimizing a Trainium2 kernel written in Bass

```python
import numpy as np
import jax
import jax.numpy as jnp

def _softmax(x, axis=-1):
    return jax.nn.softmax(x, axis=axis)

def _gelu(x):
    return jax.nn.gelu(x, approximate=True)

def _silu(x):
    return jax.nn.silu(x)

def _sigmoid(x):
    return jax.nn.sigmoid(x)

def _layernorm(x, axis=-1, eps=1e-05):
    m = jnp.mean(x, axis=axis, keepdims=True)
    v = jnp.var(x, axis=axis, keepdims=True)
    return (x - m) / jnp.sqrt(v + eps)

def _scatter_add(tgt, idx, src, axis=0):
    return tgt.at[idx].add(src)

def _segment_sum(src, seg, n):
    return jax.ops.segment_sum(src, seg, n)
kernel_name = 'mk_adaln_attn_ffn_d1_seqx_r4_afc515'

def setup_inputs(seed: int=0):
    np.random.seed(seed)
    _w = jnp.asarray

    def _rec_inputs():
        import jax
        import jax.numpy as jnp
        _rk = jax.random.key(seed)
        x = -7.109e-05 + 0.9999 * jax.random.normal(jax.random.fold_in(_rk, 1), (64, 64, 1024), jnp.float32)
        _lenS = 64 - jax.random.randint(jax.random.fold_in(_rk, 7), (64,), 0, max(1, 64 // 4) + 1, jnp.int32)
        _lenS2 = 64 - jax.random.randint(jax.random.fold_in(_rk, 8), (64,), 0, max(1, 64 // 4) + 1, jnp.int32)
        itok_B_4_50 = jax.random.randint(jax.random.fold_in(_rk, 11), (64,), 4, 51, jnp.int32)
        itok_B_0_15 = jax.random.randint(jax.random.fold_in(_rk, 12), (64,), 0, 16, jnp.int32)
        return (x, itok_B_4_50, itok_B_0_15)
    x, itok_B_4_50, itok_B_0_15 = _rec_inputs()

    def _L0_cond_setup():
        import jax, jax.numpy as jnp
        import numpy as np
        RANK = 16
        ALPHA = 16.0
        SCALING = ALPHA / RANK
        key = jax.random.key(seed)
        k1, k2, k3, k4 = jax.random.split(key, 4)
        batch, n_tok, d_in, d_out, n_adapters, rank = (8, 512, 1024, 1024, 64, RANK)
        x = jax.random.normal(k1, (batch, n_tok, d_in), dtype=jnp.float32)
        A = jax.random.normal(k2, (n_adapters, d_out, rank), dtype=jnp.float32) * 0.02
        B = jax.random.normal(k3, (n_adapters, rank, d_in), dtype=jnp.float32)
        adapter_ids = jax.random.randint(k4, (batch,), 0, n_adapters, dtype=jnp.int32)
        return {'x': x, 'A': A, 'B': B, 'adapter_ids': adapter_ids}
    _L0_cond_all = _L0_cond_setup()
    _L0_cond_in = {k: v for k, v in _L0_cond_all.items() if k in ('A', 'B')}
    del _L0_cond_all

    def _L0_attn_setup():
        import jax, jax.numpy as jnp
        import numpy as np
        import math
        FACTOR = 1
        key = jax.random.key(seed)
        x = jax.random.normal(key, (8, 128, 1024), dtype=jnp.float32)
        return {'x': x}
    _L0_attn_all = _L0_attn_setup()
    _L0_attn_in = {k: v for k, v in _L0_attn_all.items() if k in ()}
    del _L0_attn_all

    def _L0_cond2_setup():
        import jax, jax.numpy as jnp
        import numpy as np
        NUM_CONDITIONS = 16
        IN_CH = 64
        OUT_CH = 64
        B = 64
        T = 1024
        key = jax.random.key(seed)
        k_x, k_w, k_c = jax.random.split(key, 3)
        x = jax.random.normal(k_x, (B, IN_CH, T), dtype=jnp.float32)
        bound = float(np.sqrt(6.0 / IN_CH))
        weights = jax.random.uniform(k_w, (NUM_CONDITIONS, IN_CH, OUT_CH), dtype=jnp.float32, minval=-bound, maxval=bound)
        condition = jax.random.randint(k_c, (B,), 0, NUM_CONDITIONS, dtype=jnp.int64)
        return {'x': x, 'weights': weights, 'condition': condition}
    _L0_cond2_all = _L0_cond2_setup()
    _L0_cond2_in = {k: v for k, v in _L0_cond2_all.items() if k in ('weights',)}
    del _L0_cond2_all

    def _L0_ffn_setup():
        import jax, jax.numpy as jnp
        import numpy as np
        D_IN = 1024
        D_OUT = 1024
        RANK = 16
        NUM_EXPERTS = 8
        TOP_K = 2
        SCALING = 32.0 / RANK
        key = jax.random.key(seed)
        ks = jax.random.split(key, 6)
        x = jax.random.normal(ks[0], (4, 512, D_IN), dtype=jnp.float32)
        W_base = jax.random.normal(ks[1], (D_OUT, D_IN), dtype=jnp.float32) * (1.0 / np.sqrt(D_IN))
        b_base = jax.random.normal(ks[2], (D_OUT,), dtype=jnp.float32) * 0.01
        W_router = jax.random.normal(ks[3], (NUM_EXPERTS, D_IN), dtype=jnp.float32) * 0.01
        A_stack = jax.random.uniform(ks[4], (NUM_EXPERTS, RANK, D_IN), dtype=jnp.float32, minval=-1.0, maxval=1.0) * (1.0 / np.sqrt(D_IN))
        B_stack = jax.random.normal(ks[5], (NUM_EXPERTS, D_OUT, RANK), dtype=jnp.float32) * 0.02
        return {'x': x, 'W_base': W_base, 'b_base': b_base, 'W_router': W_router, 'A_stack': A_stack, 'B_stack': B_stack}
    _L0_ffn_all = _L0_ffn_setup()
    _L0_ffn_in = {k: v for k, v in _L0_ffn_all.items() if k in ('W_base', 'b_base', 'W_router', 'A_stack', 'B_stack')}
    del _L0_ffn_all
    return {'x': x, 'itok_B_4_50': itok_B_4_50, 'itok_B_0_15': itok_B_0_15, 'L0_cond_A': _L0_cond_in['A'], 'L0_cond_B': _L0_cond_in['B'], 'L0_cond2_weights': _L0_cond2_in['weights'], 'L0_ffn_W_base': _L0_ffn_in['W_base'], 'L0_ffn_b_base': _L0_ffn_in['b_base'], 'L0_ffn_W_router': _L0_ffn_in['W_router'], 'L0_ffn_A_stack': _L0_ffn_in['A_stack'], 'L0_ffn_B_stack': _L0_ffn_in['B_stack']}

def reference(x, itok_B_4_50, itok_B_0_15, L0_cond_A, L0_cond_B, L0_cond2_weights, L0_ffn_W_base, L0_ffn_b_base, L0_ffn_W_router, L0_ffn_A_stack, L0_ffn_B_stack):
    import jax
    import jax.numpy as jnp

    def _L0_cond_ref(x, A, B, adapter_ids):
        import jax, jax.numpy as jnp
        import numpy as np
        RANK = 16
        ALPHA = 16.0
        SCALING = ALPHA / RANK
        B_req = B[adapter_ids]
        A_req = A[adapter_ids]
        Bx = jnp.einsum('bni,bri->bnr', x, B_req)
        out = jnp.einsum('bnr,bor->bno', Bx, A_req)
        return out * SCALING

    def _L0_attn_ref(x):
        import jax, jax.numpy as jnp
        import numpy as np
        import math
        FACTOR = 1
        B, C, L = x.shape
        xh = x[:, None]
        f = jnp.fft.rfft(xh, axis=-1)
        corr = jnp.fft.irfft(f * jnp.conj(f), n=L, axis=-1)
        top_k = int(FACTOR * math.log(L))
        weights, delay = jax.lax.top_k(corr, top_k)
        tmp_corr = jax.nn.softmax(weights, axis=-1)
        init_index = jnp.arange(L)
        idx = (init_index[None, None, None, None, :] + delay[..., None]) % L
        pattern = jnp.take_along_axis(xh[:, :, :, None, :], idx, axis=-1)
        delays_agg = jnp.sum(pattern * tmp_corr[..., None], axis=-2)
        return delays_agg[:, 0]

    def _L0_cond2_ref(x, weights, condition):
        import jax, jax.numpy as jnp
        import numpy as np
        NUM_CONDITIONS = 16
        IN_CH = 64
        OUT_CH = 64
        B = 64
        T = 1024
        W = weights[condition]
        return jnp.einsum('bct,bcd->bdt', x, W)

    def _L0_ffn_ref(x, W_base, b_base, W_router, A_stack, B_stack):
        import jax, jax.numpy as jnp
        import numpy as np
        D_IN = 1024
        D_OUT = 1024
        RANK = 16
        NUM_EXPERTS = 8
        TOP_K = 2
        SCALING = 32.0 / RANK
        orig_shape = x.shape
        xf = x.reshape(-1, D_IN)
        logits = xf @ W_router.T
        probs = jax.nn.softmax(logits, axis=-1)
        topk_p, topk_i = jax.lax.top_k(probs, TOP_K)
        topk_p = topk_p / jnp.sum(topk_p, axis=-1, keepdims=True)
        combine = jnp.sum(jax.nn.one_hot(topk_i, NUM_EXPERTS, dtype=xf.dtype) * topk_p[..., None], axis=1)
        h = jnp.einsum('nd,erd->ner', xf, A_stack)
        h = h * combine[..., None]
        lora_out = jnp.einsum('ner,eor->no', h, B_stack) * SCALING
        base_out = xf @ W_base.T + b_base
        out = base_out + lora_out
        return out.reshape(orig_shape[:-1] + (D_OUT,))
    x = x + _L0_attn_ref(_L0_cond_ref(x, L0_cond_A, L0_cond_B, itok_B_4_50))
    x = x + _L0_ffn_ref(_L0_cond2_ref(x, L0_cond2_weights, itok_B_0_15), L0_ffn_W_base, L0_ffn_b_base, L0_ffn_W_router, L0_ffn_A_stack, L0_ffn_B_stack)
    return x

_drawn_inputs = setup_inputs


def setup_inputs(seed=0):
    import zlib

    import numpy as np

    out = dict(_drawn_inputs(seed))
    spreads = {}
    factors = {'L0_ffn_b_base': 26.829}
    for name, (base, spread) in spreads.items():
        noise = np.random.default_rng([zlib.crc32(name.encode()), seed]).standard_normal(out[name].shape)
        drawn = base * np.exp(spread * noise) if base else spread * noise
        out[name] = jnp.asarray(drawn.astype(out[name].dtype))
    for name, factor in factors.items():
        out[name] = (out[name] * factor).astype(out[name].dtype)
    return out
```

```python
from contextlib import ExitStack

import concourse.bass as bass
import numpy as np
from concourse import mybir

F32 = mybir.dt.float32
F32R = mybir.dt.float32r
I32 = mybir.dt.int32
U32 = mybir.dt.uint32
ALU = mybir.AluOpType
ACT = mybir.ActivationFunctionType

P = 128
NS, C, L = 64, 64, 1024
R = 16
E = 8
NT = NS * C // P
SPT = P // C
GS = P // R
NG = NS // GS
TPG = NT // NG
KC = L // P
Q = L // 4
H = L // 2
TR = SPT * R
STK = 3 * TR
HW = E * R + E
NCE = Q + 2
LAG = 2
U = 4
NSEL = 5
LORA_SCALE = 2.0

C_IDENT, C_MASK, C_ROW, C_IOTA = P, TR, 1, E
SMALL = C_IDENT + C_MASK + C_ROW + C_IOTA
DCOLS = 2 * NCE + 6 * Q + NCE
KCOLS = 5 * Q


def constants():
    def cos(n):
        return np.cos(2 * np.pi * (n % L) / L)

    def sin(n):
        s = np.sin(2 * np.pi * (n % L) / L)
        return np.where(n % H == 0, 0.0, s)

    i = np.arange(P)
    even = np.concatenate([2 * i, H - 2 * i])
    odd = np.concatenate([2 * i + 1, H - 1 - 2 * i])
    l = np.arange(Q)[:, None]
    ce = np.zeros((Q, NCE))
    ce[:, :Q] = cos(l * even)
    ce[:, Q] = cos(l[:, 0] * Q)
    se = sin(l * even)
    se[:, P] = sin(l[:, 0] * Q)
    se[0] = 0.0
    co = cos(l * odd)
    so = sin(l * odd)
    so[0] = sin(Q * odd)
    mid = np.zeros((P, NCE))
    mid[0, :Q] = np.rint(cos(Q * even))
    mid[0, Q] = 1.0

    def chunks(m):
        return [m[:P], m[P:]]

    dft = np.concatenate([*chunks(ce), *chunks(se), *chunks(co), *chunks(so), mid], axis=1)
    c = np.arange(Q)
    wt = np.full((P, 1), 2.0 / L)
    w0 = wt.copy()
    w0[0] = 1.0 / L
    fe, fo = 2 * i[:, None], 2 * i[:, None] + 1
    d_odd, d_even = 2 * c + 1, 2 * c + 2
    q = np.zeros((P, Q))
    q[0] = 2.0 / L * np.rint(cos(Q * d_even))
    back = np.concatenate([w0 * cos(fe * d_even), wt * cos(fo * d_even),
                           w0 * cos(fe * d_odd), wt * cos(fo * d_odd), q], axis=1)
    small = np.zeros((P, SMALL))
    small[:, :P] = np.eye(P)
    small[:, P:P + TR] = (np.arange(P)[:, None] // C) == (np.arange(TR)[None, :] // R)
    small[:, P + TR] = np.arange(P) * 2 * L + 1
    small[:, P + TR + 1:] = np.arange(E)
    return {"dft": dft.astype(np.float32), "back": back.astype(np.float32),
            "small": small.astype(np.float32)}


def build(nc, x, attn_ids, mix_ids, ad_a, ad_b, mix_w, w_base, b_base, w_router, a_stack, b_stack,
          dft, back, small, out):
    with ExitStack() as ctx:
        def sb(name, shape, dt=F32):
            return ctx.enter_context(nc.sbuf_tensor(name, shape, dt))

        ad_hi_d = nc.dram_tensor("ad_hi_d", (NS * R, 2 * L), F32, kind="Internal").ap()
        ad_lo_d = nc.dram_tensor("ad_lo_d", (NS * R, 2 * L), F32, kind="Internal").ap()
        bt_d = nc.dram_tensor("bt_d", (NG, P, TPG * KC * TR), F32, kind="Internal").ap()
        y2_d = [nc.dram_tensor(f"y2_d{u}", (P * 2 * L, 1), F32, kind="Internal").ap() for u in range(U)]

        const = sb("const", [P, SMALL])
        ident = const[:, 0:P]
        mask = const[:, P:P + TR]
        rowbase = const[:, P + TR:P + TR + 1]
        iota8 = const[:, P + TR + 1:SMALL]
        wt_hi = sb("wt_hi", [P, KC, L], F32R)
        wt_lo = sb("wt_lo", [P, KC, L], F32R)
        aw_hi = sb("aw_hi", [P, KC, HW], F32R)
        aw_lo = sb("aw_lo", [P, KC, HW], F32R)
        bs_hi = sb("bs_hi", [P, L], F32R)
        bs_lo = sb("bs_lo", [P, L], F32R)
        back_hi = sb("back_hi", [P, 5, Q], F32R)
        back_lo = sb("back_lo", [P, 5, Q], F32R)
        bias = sb("bias", [P, L])
        ids = sb("ids", [1, 2 * NS], I32)
        setup(nc, locals())
        tiles(nc, locals())


def wait_apart(eng, regs, holds, *waits):
    if all(isinstance(value, int) for _, value in waits):
        regs = []
    else:
        for reg, (_, value) in zip(regs, waits):
            eng.reg_mov(reg, value)
        eng.wait_ge(*holds)
    for n, (sem, value) in enumerate(waits):
        eng.wait_ge(sem, regs[n] if regs else value)


def setup(nc, v):
    const, ident, ids, bias = v["const"], v["ident"], v["ids"], v["bias"]
    wt_hi, wt_lo, aw_hi, aw_lo = v["wt_hi"], v["wt_lo"], v["aw_hi"], v["aw_lo"]
    bs_hi, bs_lo, back_hi, back_lo = v["bs_hi"], v["bs_lo"], v["back_hi"], v["back_lo"]
    ad_hi_d, ad_lo_d, bt_d = v["ad_hi_d"], v["ad_lo_d"], v["bt_d"]
    with ExitStack() as ctx:
        def sb(name, shape, dt=F32):
            return ctx.enter_context(nc.sbuf_tensor(name, shape, dt))

        def ps(name):
            return ctx.enter_context(nc.psum_tensor(name, [P, L], F32))

        def sem(name):
            return ctx.enter_context(nc.semaphore(name))

        dft_raw = sb("dft_raw", [P, DCOLS])
        dft_hi = sb("dft_hi", [P, DCOLS], F32R)
        dft_lo = sb("dft_lo", [P, DCOLS], F32R)
        back_raw = sb("back_raw", [P, KCOLS])
        a_raw = [sb(f"a_raw{i}", [P, GS, KC, R]) for i in range(2)]
        b_raw = [sb(f"b_raw{i}", [P, L]) for i in range(2)]
        w_raw = [sb(f"w_raw{i}", [P, L]) for i in range(2)]
        a_perm = sb("a_perm", [P, KC, P])
        at = sb("at", [P, L])
        fold1 = sb("fold1", [P, 2, H + 1])
        fold2 = sb("fold2", [P, 4, Q])
        ft_hi = sb("ft_hi", [P, KC, P], F32R)
        ft_lo = sb("ft_lo", [P, KC, P], F32R)
        bt = sb("bt", [P, TPG, KC, TR])
        g_hi = sb("g_hi", [P, 2, L], F32R)
        g_lo = sb("g_lo", [P, 2, L], F32R)
        p_a, p_b, p_c, p_w = ps("p_a"), ps("p_b"), ps("p_c"), ps("p_w")

        def cosine(m, chunk):
            return m[:, chunk * NCE:(chunk + 1) * NCE]

        def block(m, which, chunk):
            at0 = 2 * NCE + (2 * which + chunk) * Q
            return m[:, at0:at0 + Q]

        mid_row = dft_hi[:, DCOLS - NCE:DCOLS]

        small_in = sem("small_in")
        ids_in = sem("ids_in")
        dft_in = sem("dft_in")
        back_in = sem("back_in")
        st_in = sem("st_in")
        bias_in = sem("bias_in")
        a_in = [sem(f"a_in{i}") for i in range(2)]
        b_in = [sem(f"b_in{i}") for i in range(2)]
        w_in = [sem(f"w_in{i}") for i in range(2)]
        cut_hi = sem("cut_hi")
        cut_lo = sem("cut_lo")
        bst_perm = sem("bst_perm")
        a_side = sem("a_side")
        st_ps = sem("st_ps")
        st_hi = sem("st_hi")
        st_lo = sem("st_lo")
        at_ps = sem("at_ps")
        at_out = sem("at_out")
        bt_ps = sem("bt_ps")
        bt_out = sem("bt_out")
        bt_saved = sem("bt_saved")
        w_ps = sem("w_ps")
        w_hi = sem("w_hi")
        w_lo = sem("w_lo")
        f1 = sem("f1")
        f2 = sem("f2")
        ft_ps = sem("ft_ps")
        ft_h = sem("ft_h")
        ft_l = sem("ft_l")
        sp_ps = sem("sp_ps")
        g_h = sem("g_h")
        g_l = sem("g_l")
        g_saved = sem("g_saved")
        holds = (st_in, 48)
        blk = ctx.enter_context(nc.Block())

        a_st, b_st, r_st = b_raw[1], a_raw[1], w_raw[1]

        @blk.sync
        def _(sp):
            sp.dma_start(const[:, :], v["small"]).then_inc(small_in, 16)
            sp.dma_start(ids[0:1, 0:NS], v["attn_ids"].rearrange("(o n) -> o n", o=1)).then_inc(ids_in, 16)
            sp.dma_start(ids[0:1, NS:2 * NS], v["mix_ids"].rearrange("(o n) -> o n", o=1)).then_inc(ids_in, 16)
            sp.dma_start(a_st[:, :], v["a_stack"].rearrange("e r d -> (e r) d")).then_inc(st_in, 16)
            sp.dma_start(r_st[0:E, :], v["w_router"]).then_inc(st_in, 16)
            sp.dma_start(b_st[:, :, :, :].rearrange("p e j r -> p e (j r)"),
                         v["b_stack"].rearrange("e (p j) r -> p e (j r)", p=P)).then_inc(st_in, 16)
            sp.wait_ge(ids_in, 32)
            a_src = v["ad_a"].rearrange("n (p j) r -> n p (j r)", p=P)
            w_src = v["w_base"].rearrange("(m p) i -> m p i", p=P)
            raw_a = [t[:, :, :, :].rearrange("p s j r -> p s (j r)") for t in a_raw]

            def load(g, k):
                for s in range(GS):
                    n = sp.value_load(ids[0:1, bass.ds(g * GS + s, 1)], min_val=0, max_val=NS - 1)
                    sp.dma_start(raw_a[k][:, s, :], a_src[bass.ds(n, 1)].rearrange("o p f -> (o p) f")
                                 ).then_inc(a_in[k], 16)
                    sp.dma_start(b_raw[k][s * R:(s + 1) * R, :],
                                 v["ad_b"][bass.ds(n, 1)].rearrange("o r l -> (o r) l")
                                 ).then_inc(b_in[k], 16)
                sp.dma_start(w_raw[k][:, :], w_src[bass.ds(g, 1)].rearrange("o p i -> (o p) i")
                             ).then_inc(w_in[k], 16)

            def save(g):
                sp.wait_ge(bt_out, g + 1)
                sp.dma_start(bt_d[bass.ds(g, 1)].rearrange("o p f -> (o p) f"),
                             bt[:, :, :, :].rearrange("p q k c -> p (q k c)")).then_inc(bt_saved, 16)
                rows = bass.ds(g * P, P)
                sp.wait_ge(g_h, 2 * g + 2)
                sp.dma_start(ad_hi_d[rows, :], g_hi[:, :, :].bitcast(F32).rearrange("p a l -> p (a l)")).then_inc(g_saved, 16)
                sp.wait_ge(g_l, 2 * g + 2)
                sp.dma_start(ad_lo_d[rows, :], g_lo[:, :, :].bitcast(F32).rearrange("p a l -> p (a l)")).then_inc(g_saved, 16)

            load(0, 0)
            sp.dma_start(dft_raw[:, :], v["dft"]).then_inc(dft_in, 16)
            sp.dma_start(back_raw[:, :], v["back"]).then_inc(back_in, 16)
            sp.dma_start(bias[:, :], v["b_base"].rearrange("(o n) -> o n", o=1).broadcast_to([P, L])
                         ).then_inc(bias_in, 16)
            sp.wait_ge(st_ps, 2)
            load(1, 1)
            save(0)
            with sp.Fori(0, NG // 2 - 1) as i:
                for k in range(2):
                    g = 2 * i + k
                    sp.wait_ge(a_side, g + 1)
                    sp.wait_ge(bt_ps, g + 1)
                    sp.wait_ge(w_ps, g + 1)
                    load(g + 2, k)
                    save(g + 1)
            save(NG - 1)
            sp.wait_ge(bias_in, 16)
            sp.wait_ge(bt_saved, 16 * NG)
            sp.wait_ge(g_saved, 32 * NG)

        @blk.tensor
        def _(pe):
            pe.wait_ge(small_in, 16)
            pe.wait_ge(st_in, 48)
            for k in range(KC):
                half = (k // 3) * 512 + (k % 3) * HW
                dst = (p_a if k < 6 else p_b)[:, half % L:half % L + HW]
                pe.transpose(dst[:, 0:P], a_st[:, k * P:(k + 1) * P], ident)
                last = pe.transpose(dst[:, P:HW], r_st[0:E, k * P:(k + 1) * P], ident[0:E, 0:E])
            last.then_inc(st_ps, 1)
            for j in range(KC):
                if j == 0:
                    pe.wait_ge(bst_perm, 1)
                last = pe.transpose(p_c[:, j * P:(j + 1) * P], a_perm[:, j, :], ident)
            last.then_inc(st_ps, 1)

            def body(g, use, k, first):
                pe.wait_ge(a_side, g + 1)
                if first:
                    pe.wait_ge(st_hi, 2)
                    pe.wait_ge(st_lo, 2)
                else:
                    pe.wait_ge(ft_h, g)
                    pe.wait_ge(ft_l, g)
                for j in range(KC):
                    last = pe.transpose(p_a[:, j * P:(j + 1) * P], a_perm[:, j, :], ident)
                last.then_inc(at_ps, 1)
                pe.wait_ge(b_in[k], use * 16 * GS)
                if not first:
                    pe.wait_ge(bt_out, g)
                for j in range(KC):
                    last = pe.transpose(p_b[:, j * P:(j + 1) * P], b_raw[k][:, j * P:(j + 1) * P], ident)
                last.then_inc(bt_ps, 1)
                pe.wait_ge(w_in[k], use * 16)
                if not first:
                    pe.wait_ge(w_hi, g)
                    pe.wait_ge(w_lo, g)
                for j in range(KC):
                    last = pe.transpose(p_w[:, j * P:(j + 1) * P], w_raw[k][:, j * P:(j + 1) * P], ident)
                last.then_inc(w_ps, 1)
                pe.wait_ge(f2, 8 * g + 8)
                for j in range(KC):
                    src = fold2[:, j // 2, (j % 2) * P:(j % 2 + 1) * P]
                    last = pe.transpose(p_a[:, j * P:(j + 1) * P], src, ident)
                last.then_inc(ft_ps, 1)
                pe.wait_ge(ft_h, g + 1)
                pe.wait_ge(ft_l, g + 1)
                if first:
                    pe.wait_ge(cut_hi, 1)
                    pe.wait_ge(cut_lo, 1)
                    pe.wait_ge(st_hi, 3)
                    pe.wait_ge(st_lo, 3)
                else:
                    pe.wait_ge(g_h, 2 * g)
                    pe.wait_ge(g_l, 2 * g)

                def three(dst, c, mat, start, last=False):
                    n = 0
                    for s, m in ((ft_hi, dft_hi), (ft_hi, dft_lo), (ft_lo, dft_hi)):
                        ins = pe.matmul(dst, s[:, c, :], mat(m), start=start and n == 0,
                                        stop=last and n == 2, skip_group_check=True)
                        n += 1
                    return ins

                ev, od = p_c[:, 0:512], p_c[:, 512:1024]
                three(ev[:, 0:NCE], 0, lambda m: cosine(m, 0), True)
                three(ev[:, 0:NCE], 1, lambda m: cosine(m, 1), False)
                for s in (ft_hi, ft_lo):
                    pe.matmul(ev[:, 0:NCE], s[:, 4, :], mid_row, start=False, stop=False,
                              skip_group_check=True)
                three(ev[:, Q:2 * Q], 4, lambda m: block(m, 0, 0), False)
                three(ev[:, Q:2 * Q], 5, lambda m: block(m, 0, 1), False, True)
                three(od[:, 0:Q], 2, lambda m: block(m, 1, 0), True)
                three(od[:, 0:Q], 3, lambda m: block(m, 1, 1), False)
                three(od[:, Q:2 * Q], 6, lambda m: block(m, 2, 0), False)
                three(od[:, Q:2 * Q], 7, lambda m: block(m, 2, 1), False, True).then_inc(sp_ps, 1)

            body(0, 1, 0, True)
            body(1, 1, 1, False)
            with pe.Fori(1, NG // 2) as i:
                for k in range(2):
                    body(2 * i + k, i + 1, k, False)

        def stacks(eng, copy, done, part):
            aw = (aw_hi, aw_lo)[part]
            if part == 0:
                eng.wait_ge(st_ps, 1)
            else:
                eng.wait_ge(st_hi, 2)
            copy(aw[:, 0:3, :], p_a[:, 0:3 * HW].rearrange("p (k c) -> p k c", k=3), aw_hi[:, 0:3, :])
            copy(aw[:, 3:6, :], p_a[:, 512:512 + 3 * HW].rearrange("p (k c) -> p k c", k=3), aw_hi[:, 3:6, :]
                 ).then_inc(done, 1)
            copy(aw[:, 6:8, :], p_b[:, 0:2 * HW].rearrange("p (k c) -> p k c", k=2), aw_hi[:, 6:8, :]
                 ).then_inc(done, 1)
            eng.wait_ge(*((st_ps, 2) if part == 0 else (st_hi, 3)))
            bs = (bs_hi, bs_lo)[part]
            copy(bs[:, :].rearrange("q (p j) -> q j p", j=KC), p_c[:, :].rearrange("q (j p) -> q j p", j=KC),
                 bs_hi[:, :].rearrange("q (p j) -> q j p", j=KC)).then_inc(done, 1)

        @blk.scalar
        def _(act):
            def copy(dst, src, _=None):
                return act.activation(dst, src, ACT.Copy)

            stacks(act, copy, st_hi, 0)
            act.wait_ge(dft_in, 16)
            copy(dft_hi[:, :], dft_raw[:, :]).then_inc(cut_hi, 1)
            act.wait_ge(back_in, 16)
            copy(back_hi[:, :, :].rearrange("p a c -> p (a c)"), back_raw[:, :]).then_inc(cut_hi, 1)

            def body(g, first):
                act.wait_ge(at_ps, g + 1)
                if not first:
                    act.wait_ge(f1, 3 * g)
                    act.wait_ge(g_h, 2 * g)
                    act.wait_ge(g_l, 2 * g)
                for b in range(2):
                    dst = at[:, :].rearrange("q (p j) -> q j p", j=KC)[:, 4 * b:4 * b + 4, :]
                    copy(dst, p_a[:, b * 512:(b + 1) * 512].rearrange("q (j p) -> q j p", j=4)
                         ).then_inc(at_out, 1)
                act.wait_ge(at_out, 2 * g + 2)
                if not first:
                    act.wait_ge(g_saved, 32 * g)
                copy(g_hi[:, 0, :], at[:, :]).then_inc(g_h, 1)
                act.wait_ge(w_ps, g + 1)
                copy(wt_hi[:, :, bass.ds(g * P, P)], p_w[:, :].rearrange("p (k o) -> p k o", k=KC)
                     ).then_inc(w_hi, 1)
                act.wait_ge(ft_ps, g + 1)
                copy(ft_hi[:, :, :].rearrange("p k c -> p (k c)"), p_a[:, :]).then_inc(ft_h, 1)
                act.wait_ge(sp_ps, g + 1)
                copy(g_hi[:, 1, :], p_c[:, :]).then_inc(g_h, 1)

            body(0, True)
            with act.Fori(1, NG) as g:
                body(g, False)

        @blk.vector
        def _(dve):
            def low(dst, src, hi):
                return dve.tensor_tensor(dst, src, hi.bitcast(F32), ALU.subtract)

            stacks(dve, low, st_lo, 1)
            dve.wait_ge(cut_hi, 1)
            low(dft_lo[:, :], dft_raw[:, :], dft_hi[:, :]).then_inc(cut_lo, 1)
            dve.wait_ge(cut_hi, 2)
            low(back_lo[:, :, :].rearrange("p a c -> p (a c)"), back_raw[:, :],
                back_hi[:, :, :].rearrange("p a c -> p (a c)")).then_inc(cut_lo, 1)

            def body(g, first):
                dve.wait_ge(bt_ps, g + 1)
                if not first:
                    dve.wait_ge(bt_saved, 16 * g)
                dve.tensor_copy(bt[:, :, :, :].rearrange("p q k c -> p k q c"),
                                p_b[:, :].rearrange("p (k q c) -> p k q c", k=KC, q=TPG)).then_inc(bt_out, 1)
                dve.wait_ge(g_h, 2 * g + 1)
                if not first:
                    dve.wait_ge(g_saved, 32 * g)
                low(g_lo[:, 0, :], at[:, :], g_hi[:, 0, :]).then_inc(g_l, 1)
                dve.wait_ge(w_hi, g + 1)
                low(wt_lo[:, :, bass.ds(g * P, P)], p_w[:, :].rearrange("p (k o) -> p k o", k=KC),
                    wt_hi[:, :, bass.ds(g * P, P)]).then_inc(w_lo, 1)
                dve.wait_ge(ft_h, g + 1)
                low(ft_lo[:, :, :].rearrange("p k c -> p (k c)"), p_a[:, :],
                    ft_hi[:, :, :].rearrange("p k c -> p (k c)")).then_inc(ft_l, 1)
                dve.wait_ge(g_h, 2 * g + 2)
                low(g_lo[:, 1, :], p_c[:, :], g_hi[:, 1, :]).then_inc(g_l, 1)

            body(0, True)
            with dve.Fori(1, NG) as g:
                body(g, False)

        @blk.gpsimd
        def _(pool):
            regs = [pool.alloc_register(f"pool_setup_wait{n}") for n in range(2)]

            def side_by_side(raw):
                return pool.tensor_copy(a_perm[:, :, :].rearrange("p j (s r) -> p j s r", s=GS),
                                        raw[:, :, :, :].rearrange("p s j r -> p j s r"))

            pool.wait_ge(st_in, 48)
            side_by_side(b_st).then_inc(bst_perm, 1)

            def body(g, use, k, first):
                wait_apart(pool, regs, holds, (a_in[k], use * 16 * GS), (st_ps, 2) if first else (at_ps, g))
                side_by_side(a_raw[k]).then_inc(a_side, 1)
                pool.wait_ge(at_out, 2 * g + 2)
                fwd, rev = at[:, 1:H], at[:, L - 1:H:-1]
                pool.tensor_tensor(fold1[:, 0, 1:H], fwd, rev, ALU.add).then_inc(f1, 1)
                pool.tensor_tensor(fold1[:, 1, 1:H], fwd, rev, ALU.subtract).then_inc(f1, 1)
                pool.tensor_copy(fold1[:, 0, 0:H + 1:H], at[:, 0:H + 1:H]).then_inc(f1, 1)
                wait_apart(pool, regs, holds, (f1, 3 * g + 3))
                if not first:
                    pool.wait_ge(ft_ps, g)
                s, d = fold1[:, 0, :], fold1[:, 1, :]
                pool.tensor_tensor(fold2[:, 0, :], s[:, 0:Q], s[:, H:Q:-1], ALU.add).then_inc(f2, 2)
                pool.tensor_tensor(fold2[:, 1, :], s[:, 0:Q], s[:, H:Q:-1], ALU.subtract).then_inc(f2, 2)
                pool.tensor_tensor(fold2[:, 2, 1:Q], d[:, 1:Q], d[:, H - 1:Q:-1], ALU.subtract).then_inc(f2, 1)
                pool.tensor_tensor(fold2[:, 3, 1:Q], d[:, 1:Q], d[:, H - 1:Q:-1], ALU.add).then_inc(f2, 1)
                pool.tensor_copy(fold2[:, 2:4, 0:1], fold1[:, :, Q:Q + 1]).then_inc(f2, 2)

            body(0, 1, 0, True)
            body(1, 1, 1, False)
            with pool.Fori(1, NG // 2) as i:
                for k in range(2):
                    body(2 * i + k, i + 1, k, False)


def tiles(nc, v):
    x, out, y2_d = v["x"], v["out"], v["y2_d"]
    ident, mask, rowbase, iota8 = v["ident"], v["mask"], v["rowbase"], v["iota8"]
    ids, bias = v["ids"], v["bias"]
    wt_hi, wt_lo, aw_hi, aw_lo = v["wt_hi"], v["wt_lo"], v["aw_hi"], v["aw_lo"]
    bs_hi, bs_lo, back_hi, back_lo = v["bs_hi"], v["bs_lo"], v["back_hi"], v["back_lo"]
    ad_hi_d, ad_lo_d, bt_d = v["ad_hi_d"], v["ad_lo_d"], v["bt_d"]
    with ExitStack() as ctx:
        def sb(name, shape, dt=F32):
            return ctx.enter_context(nc.sbuf_tensor(name, shape, dt))

        def ps(name, cols):
            return ctx.enter_context(nc.psum_tensor(name, [P, cols], F32))

        def sem(name):
            return ctx.enter_context(nc.semaphore(name))

        row = [sb(f"row{u}", [P, L]) for u in range(U)]
        adapter = [sb(f"adapter{k}", [STK, 2 * L], F32R) for k in range(2)]
        bt = [sb(f"btile{u}", [P, KC, TR]) for u in range(U)]
        mix = [sb(f"mix{u}", [P, P]) for u in range(U)]
        xt = sb("xt", [P, KC, P])
        bx = sb("bx", [P, TR])
        bx_hi = sb("bx_hi", [P, TR], F32R)
        bx_stack = sb("bx_stack", [P, STK])
        s_t = sb("s_t", [STK, P], F32R)
        sq = sb("sq", [P, 2, 2, 2, P])
        pw = sb("pw", [P, 2, 2 * P])
        eo = sb("eo", [P, 5, P])
        eo_hi = sb("eo_hi", [P, 5, P], F32R)
        eo_lo = sb("eo_lo", [P, 5, P], F32R)
        y = [sb(f"y{k}", [P, L]) for k in range(2)]
        corr0 = [sb(f"corr0_{k}", [P, 1]) for k in range(2)]
        rolled = [sb(f"rolled{n}", [P, L]) for n in range(NSEL)]
        val = sb("val", [P, 8])
        idx = sb("idx", [P, 8], U32)
        is_mid = sb("is_mid", [P, 2])
        not_mid = sb("not_mid", [P, 2])
        part = sb("part", [P, 2])
        in_even = sb("in_even", [P, 3])
        delay = sb("delay", [P, NSEL])
        mirror = sb("mirror", [P, 3])
        off = sb("off", [P, NSEL], U32)
        neg_max = sb("neg_max", [P, 1])
        ex = sb("ex", [P, NSEL + 1])
        ex_sum = sb("ex_sum", [P, 1])
        ex_inv = sb("ex_inv", [P, 1])
        weight = sb("weight", [P, NSEL + 1])
        rval = sb("rval", [P, 8])
        ridx = sb("ridx", [P, 8], U32)
        ridx_f = sb("ridx_f", [P, 2])
        rneg = sb("rneg", [P, 1])
        rex = sb("rex", [P, 2])
        rsum = sb("rsum", [P, 1])
        rinv = sb("rinv", [P, 1])
        rp = sb("rp", [P, 2])
        comb = sb("comb", [P, 2, E])
        combine = sb("combine", [P, E])
        hc = sb("hc", [P, P])
        ht_hi = sb("ht_hi", [P, P], F32R)
        ht_lo = sb("ht_lo", [P, P], F32R)
        x2_hi = sb("x2_hi", [P, KC, P], F32R)
        x2_lo = sb("x2_lo", [P, KC, P], F32R)
        t_ps, x_ps, o_ps = ps("t_ps", L), ps("x_ps", L), ps("o_ps", L)
        h_ps, c_ps = ps("h_ps", 512), ps("c_ps", 512)
        ht_ps = h_ps[:, 256:256 + P]
        bx_ps = x_ps[:, 0:TR]
        s_ps = x_ps[0:STK, 512:512 + P]

        row_in = [sem(f"row_in{u}") for u in range(U)]
        mix_in = [sem(f"mix_in{u}") for u in range(U)]
        bt_in = [sem(f"bt_in{u}") for u in range(U)]
        adapter_in = [sem(f"adapter_in{k}") for k in range(2)]
        y_saved = [sem(f"y_saved{k}") for k in range(2)]
        rolled_in = [sem(f"rolled_in{n}") for n in range(NSEL)]
        out_saved = [sem(f"out_saved{u}") for u in range(U)]
        xt_ps = sem("xt_ps")
        bx_mm = sem("bx_mm")
        s_mm = sem("s_mm")
        spec_mm = sem("spec_mm")
        y_mm = sem("y_mm")
        corr_mm = sem("corr_mm")
        x2_mm = sem("x2_mm")
        h_mm = sem("h_mm")
        ht_mm = sem("ht_mm")
        out_mm = sem("out_mm")
        xt_out = sem("xt_out")
        s_out = sem("s_out")
        sq_out = sem("sq_out")
        y_out = sem("y_out")
        y_free = sem("y_free")
        eo_h = sem("eo_h")
        exp_out = sem("exp_out")
        rexp_out = sem("rexp_out")
        ht_h = sem("ht_h")
        x2_h = sem("x2_h")
        bx_step = sem("bx_step")
        eo_l = sem("eo_l")
        top_step = sem("top_step")
        w_step = sem("w_step")
        sum_step = sem("sum_step")
        r_step = sem("r_step")
        hc_out = sem("hc_out")
        ht_l = sem("ht_l")
        x2_l = sem("x2_l")
        out_add = sem("out_add")
        cleared = sem("cleared")
        biased = sem("biased")
        fold_step = sem("fold_step")
        blk = ctx.enter_context(nc.Block())
        TOPS, RS, BXS, FS = 14, 9, 4, 6
        SUMS = NSEL + 1
        holds = (cleared, 1)

        def slots(eng, slot):
            for s in range(U):
                slot(s, s % U, s // U)
            with eng.Fori(1, NT // U) as i:
                for u in range(U):
                    slot(i * U + u, u, i)
            for s in range(NT, NT + LAG):
                slot(s, s % U, s // U)

        def has_attn(s):
            return not isinstance(s, int) or s < NT

        def has(t):
            return not isinstance(t, int) or 0 <= t < NT

        def from_first(t):
            return not isinstance(t, int) or t > 0

        def uses(t, u, i, ring):
            return (U // ring) * i + u // ring + 1

        def before(u, i, n):
            return ((u - n) % U, i + (u - n) // U)

        @blk.sync
        def _(sp):
            x_t = x.rearrange("(t b) c l -> t (b c) l", b=SPT)
            out_t = out.rearrange("(t b) c l -> t (b c) l", b=SPT)
            bt_t = bt_d.rearrange("g p (q f) -> g q p f", q=TPG)

            def load(t, u, i):
                if isinstance(t, int) and t >= NT:
                    return
                if not isinstance(t, int) or t >= U:
                    sp.wait_ge(out_saved[u], i * 16)
                sp.dma_start(row[u][:, :], x_t[bass.ds(t, 1)].rearrange("o p l -> (o p) l")
                             ).then_inc(row_in[u], 16)
                sp.dma_start(bt[u][:, :, :].rearrange("p k c -> p (k c)"),
                             bt_t[bass.ds(i, 1), u].rearrange("o p f -> (o p) f")).then_inc(bt_in[u], 16)
                if not isinstance(t, int) or t >= 2:
                    sp.wait_ge(y_mm, t - 1)
                k = u % 2
                for n, src in enumerate((ad_hi_d, ad_lo_d, ad_hi_d)):
                    sp.dma_start(adapter[k][n * TR:(n + 1) * TR, :].bitcast(F32), src[bass.ds(t * TR, TR), :]
                                 ).then_inc(adapter_in[k], 16)
                for b in range(SPT):
                    n = sp.value_load(ids[0:1, bass.ds(t * SPT + b + NS, 1)], min_val=0,
                                      max_val=v["mix_w"].shape[0] - 1)
                    sp.dma_start(mix[u][b * C:(b + 1) * C, b * C:(b + 1) * C],
                                 v["mix_w"][bass.ds(n, 1)].rearrange("o c d -> (o c) d")
                                 ).then_inc(mix_in[u], 16)

            def slot(s, u, i):
                un, in_ = (u + 1) % U, i + (u + 1) // U
                load(s + 1, un, in_)
                if has_attn(s):
                    sp.wait_ge(y_out, s + 1)
                    y2 = y2_d[u].rearrange("(p l) o -> p (l o)", p=P)
                    for h in range(2):
                        sp.dma_start(y2[:, h * L:(h + 1) * L], y[u % 2][:, :]).then_inc(y_saved[u % 2], 16)
                t = s - LAG
                if has(t):
                    ut, it = before(u, i, LAG)
                    sp.wait_ge(out_add, t + 1)
                    sp.dma_start(out_t[bass.ds(t, 1)].rearrange("o p l -> (o p) l"), row[ut][:, :]
                                 ).then_inc(out_saved[ut], 16)

            sp.wait_ge(cleared, 1)
            load(0, 0, 0)
            for s in range(U):
                slot(s, s % U, s // U)
            with sp.Fori(1, NT // U - 1) as i:
                for u in range(U):
                    slot(i * U + u, u, i)
            for s in range(NT - U, NT + LAG):
                slot(s, s % U, s // U)
            for u in range(U):
                sp.wait_ge(out_saved[u], 16 * NT // U)

        @blk.tensor
        def _(pe):
            def three(dst, pairs, start, stop):
                n, last = 0, None
                todo = [(a, b) for (ah, al), (bh, bl) in pairs for a, b in ((ah, bh), (ah, bl), (al, bh))]
                for a, b in todo:
                    last = pe.matmul(dst, a, b, start=start and n == 0, stop=stop and n == len(todo) - 1)
                    n += 1
                return last

            def x_transposed(s, u, i, half):
                if half == 0:
                    pe.wait_ge(row_in[u], (i + 1) * 16)
                    if from_first(s):
                        pe.wait_ge(y_free, s)
                for c in range(4 * half, 4 * half + 4):
                    last = pe.transpose(t_ps[:, c * P:(c + 1) * P], row[u][:, c * P:(c + 1) * P], ident)
                last.then_inc(xt_ps, 1)

            def b_times_x(s, u, i):
                pe.wait_ge(bt_in[u], (i + 1) * 16)
                pe.wait_ge(xt_out, 2 * s + 2)
                if not isinstance(s, int) or s >= LAG:
                    pe.wait_ge(x2_l, 2 * s - 2)
                    pe.wait_ge(x2_h, 2 * s - 2)
                for c in range(KC):
                    last = pe.matmul(bx_ps, xt[:, c, :], bt[u][:, c, :], start=c == 0, stop=c == KC - 1)
                last.then_inc(bx_mm, 1)

            def stack_transposed(s):
                pe.wait_ge(bx_step, BXS * s + BXS)
                pe.transpose(s_ps, bx_stack[:, :], ident).then_inc(s_mm, 1)

            def spectrum(s, u, i):
                pe.wait_ge(adapter_in[u % 2], uses(s, u, i, 2) * 48)
                pe.wait_ge(s_out, s + 1)
                for c in range(KC):
                    last = pe.matmul(t_ps[:, c * P:(c + 1) * P], adapter[u % 2][:, L + c * P:L + (c + 1) * P],
                                     s_t[:, :], start=True, stop=True)
                last.then_inc(spec_mm, 1)

            def adapter_out(s, u):
                pe.wait_ge(sq_out, s + 1)
                for h in range(2):
                    last = pe.matmul(t_ps[:, h * 512:(h + 1) * 512], s_t[:, :],
                                     adapter[u % 2][:, h * 512:(h + 1) * 512], start=True, stop=True)
                last.then_inc(y_mm, 1)

            def correlation(s):
                pe.wait_ge(eo_h, s + 1)
                pe.wait_ge(eo_l, s + 1)
                if from_first(s):
                    pe.wait_ge(top_step, TOPS * s)
                def pair(n):
                    return (eo_hi[:, n, :], eo_lo[:, n, :]), (back_hi[:, n, :], back_lo[:, n, :])
                three(c_ps[:, 0:Q], [pair(2), pair(3)], True, True)
                three(c_ps[:, Q:2 * Q], [pair(0), pair(1)], True, False)
                pe.matmul(c_ps[:, Q:2 * Q], eo_hi[:, 4, :], back_hi[:, 4, :], start=False, stop=False)
                pe.matmul(c_ps[:, Q:2 * Q], eo_lo[:, 4, :], back_hi[:, 4, :], start=False, stop=True
                          ).then_inc(corr_mm, 1)

            def mixed(t, u, i):
                pe.wait_ge(mix_in[u], (i + 1) * 32)
                pe.wait_ge(sum_step, SUMS * t + SUMS)
                if has(t + 1):
                    pe.wait_ge(bx_step, BXS * (t + 1) + 1)
                    pe.wait_ge(s_out, t + 2)
                for c in range(KC):
                    last = pe.matmul(x_ps[:, c * P:(c + 1) * P], row[u][:, c * P:(c + 1) * P], mix[u][:, :],
                                     start=True, stop=True)
                    if c % 4 == 3:
                        last.then_inc(x2_mm, 1)

            def project(t):
                pe.wait_ge(x2_h, 2 * t + 2)
                pe.wait_ge(x2_l, 2 * t + 2)
                if from_first(t):
                    pe.wait_ge(ht_h, t)
                    pe.wait_ge(ht_l, t)
                three(h_ps[:, 0:HW], [((x2_hi[:, c, :], x2_lo[:, c, :]), (aw_hi[:, c, :], aw_lo[:, c, :]))
                                      for c in range(KC)], True, True).then_inc(h_mm, 1)

            def h_transposed(t):
                pe.wait_ge(hc_out, t + 1)
                pe.transpose(ht_ps, hc[:, :], ident).then_inc(ht_mm, 1)

            def base(t, c):
                if c == 0 and from_first(t):
                    pe.wait_ge(out_add, t)
                for h in range(2):
                    cols = slice(h * 512, (h + 1) * 512)
                    three(o_ps[:, cols], [((x2_hi[:, c, :], x2_lo[:, c, :]),
                                           (wt_hi[:, c, cols], wt_lo[:, c, cols]))], c == 0, False)

            def experts(t):
                pe.wait_ge(ht_h, t + 1)
                pe.wait_ge(ht_l, t + 1)
                for h in range(2):
                    cols = slice(h * 512, (h + 1) * 512)
                    last = three(o_ps[:, cols], [((ht_hi[:, :], ht_lo[:, :]), (bs_hi[:, cols], bs_lo[:, cols]))],
                                 False, True)
                last.then_inc(out_mm, 1)

            def slot(s, u, i):
                t = s - LAG
                attn = has_attn(s)
                steps = [lambda: attn and x_transposed(s, u, i, 0),
                         lambda: attn and x_transposed(s, u, i, 1),
                         lambda: attn and b_times_x(s, u, i),
                         lambda: has(t) and h_transposed(t),
                         lambda: attn and stack_transposed(s),
                         lambda: attn and spectrum(s, u, i),
                         lambda: attn and adapter_out(s, u),
                         lambda: None]
                if has(t):
                    project(t)
                for c in range(KC):
                    if has(t):
                        base(t, c)
                    steps[c]()
                if has(t):
                    experts(t)
                if has(s - 1):
                    mixed(s - 1, *before(u, i, 1))
                if attn:
                    correlation(s)

            slots(pe, slot)

        @blk.scalar
        def _(act):
            def slot(s, u, i):
                t, last = s - LAG, s - 1
                if has(last):
                    act.wait_ge(top_step, TOPS * last + TOPS)
                    act.activation(ex[:, :], val[:, 0:NSEL + 1], ACT.Exp, bias=neg_max[:, :],
                                   accum_out=ex_sum[:, :]).then_inc(exp_out, 1)
                if has(t):
                    act.wait_ge(r_step, RS * t + 3)
                    act.activation(rex[:, :], rval[:, 0:2], ACT.Exp, bias=rneg[:, :],
                                   accum_out=rsum[:, :]).then_inc(rexp_out, 1)
                if has_attn(s):
                    for h in range(2):
                        act.wait_ge(xt_ps, 2 * s + 1 + h)
                        if h == 0 and from_first(s):
                            act.wait_ge(bx_mm, s)
                        act.activation(xt[:, 4 * h:4 * h + 4, :].rearrange("p k c -> p (k c)"),
                                       t_ps[:, h * 512:(h + 1) * 512], ACT.Copy).then_inc(xt_out, 1)
                if has(t):
                    act.wait_ge(ht_mm, t + 1)
                    if from_first(t):
                        act.wait_ge(out_mm, t)
                    act.activation(ht_hi[:, :], ht_ps, ACT.Copy).then_inc(ht_h, 1)
                if has_attn(s):
                    act.wait_ge(s_mm, s + 1)
                    if from_first(s):
                        act.wait_ge(y_mm, s)
                    act.activation(s_t[:, :], s_ps, ACT.Copy).then_inc(s_out, 1)
                    act.wait_ge(spec_mm, s + 1)
                    if from_first(s):
                        act.wait_ge(fold_step, FS * s)
                    act.activation(sq[:, :, :, :, :].rearrange("p a b h r -> p (a b h r)"), t_ps[:, :],
                                   ACT.Square).then_inc(sq_out, 1)
                    act.wait_ge(y_mm, s + 1)
                    k = u % 2
                    if not isinstance(s, int) or s >= 2:
                        act.wait_ge(sum_step, SUMS * (s - 2) + 1)
                        act.wait_ge(y_saved[k], 32 * (uses(s, u, i, 2) - 1))
                    act.activation(y[k][:, :], t_ps[:, :], ACT.Copy).then_inc(y_out, 1)
                    act.wait_ge(y_out, s + 1)
                    act.activation(t_ps[:, :], y[k][:, :], ACT.Square, accum_out=corr0[k][:, :]).then_inc(y_free, 1)
                    act.wait_ge(fold_step, FS * s + FS)
                    if from_first(s):
                        act.wait_ge(corr_mm, s)
                        act.wait_ge(eo_l, s)
                    act.activation(eo_hi[:, :, :].rearrange("p a r -> p (a r)"),
                                   eo[:, :, :].rearrange("p a r -> p (a r)"), ACT.Copy).then_inc(eo_h, 1)
                if has(last):
                    for h in range(2):
                        act.wait_ge(x2_mm, 2 * last + 1 + h)
                        act.activation(x2_hi[:, 4 * h:4 * h + 4, :].rearrange("p k r -> p (k r)"),
                                       x_ps[:, h * 512:(h + 1) * 512], ACT.Copy).then_inc(x2_h, 1)

            slots(act, slot)

        @blk.vector
        def _(dve):
            regs = [dve.alloc_register(f"dve_wait{n}") for n in range(2)]

            def top_delays(s, k):
                n = [TOPS * s]

                def step(ins, wait=True):
                    ins.then_inc(top_step, 1)
                    n[0] = n[0] + 1
                    if wait:
                        dve.wait_ge(top_step, n[0])

                corr = c_ps[:, :]
                wait_apart(dve, regs, holds, (corr_mm, s + 1), *([(exp_out, s)] if from_first(s) else []))
                step(dve.max(val[:, :], corr), False)
                wait_apart(dve, regs, holds, (top_step, n[0]))
                step(dve.max_index(idx[:, :], val[:, :], corr))
                step(dve.tensor_scalar(in_even[:, :], idx[:, 0:3], float(Q), 1.0 - H, ALU.is_ge, ALU.mult))
                step(dve.scalar_tensor_tensor(delay[:, 0:3], idx[:, 0:3], 2.0, in_even[:, :], ALU.mult, ALU.add))
                step(dve.tensor_scalar(is_mid[:, :], idx[:, 0:2], float(H - 1), None, ALU.is_equal), False)
                step(dve.tensor_scalar(not_mid[:, :], idx[:, 0:2], float(H - 1), None, ALU.not_equal), False)
                step(dve.tensor_scalar(mirror[:, :], delay[:, 0:3], -1.0, float(L - 2), ALU.mult, ALU.add))
                step(dve.tensor_tensor(part[:, :], mirror[:, 0:2], not_mid[:, :], ALU.mult))
                step(dve.scalar_tensor_tensor(delay[:, 3:5], is_mid[:, :], mirror[:, 2:3], part[:, :],
                                              ALU.mult, ALU.add))
                if from_first(s):
                    for m in range(NSEL):
                        dve.wait_ge(rolled_in[m], 16 * s)
                step(dve.tensor_scalar(off[:, :], delay[:, :], rowbase, None, ALU.add), False)
                step(dve.tensor_tensor(part[:, :], val[:, 0:2], not_mid[:, :], ALU.mult))
                dve.wait_ge(y_free, s + 1)
                step(dve.tensor_scalar(neg_max[:, :], val[:, 0:1], corr0[k][:, :], -1.0, ALU.max, ALU.mult), False)
                step(dve.scalar_tensor_tensor(val[:, 3:5], is_mid[:, :], val[:, 2:3], part[:, :],
                                              ALU.mult, ALU.add), False)
                step(dve.tensor_copy(val[:, 5:6], corr0[k][:, :]), False)

            def weights(s):
                dve.wait_ge(exp_out, s + 1)
                dve.reciprocal(ex_inv[:, :], ex_sum[:, :]).then_inc(w_step, 1)
                dve.wait_ge(w_step, 2 * s + 1)
                if from_first(s):
                    dve.wait_ge(sum_step, SUMS * s)
                dve.tensor_scalar(weight[:, :], ex[:, :], ex_inv[:, :], None, ALU.mult).then_inc(w_step, 1)
                dve.wait_ge(w_step, 2 * s + 2)

            def add_y(s, u):
                dve.scalar_tensor_tensor(row[u][:, :], y[u % 2][:, :], weight[:, 5:6], row[u][:, :],
                                         ALU.mult, ALU.add).then_inc(sum_step, 1)

            def add_rolled(s, u, n):
                dve.wait_ge(rolled_in[n], 16 * (s + 1))
                dve.wait_ge(sum_step, SUMS * s + n + 1)
                dve.scalar_tensor_tensor(row[u][:, :], rolled[n][:, :], weight[:, n:n + 1], row[u][:, :],
                                         ALU.mult, ALU.add).then_inc(sum_step, 1)

            def router(t):
                n = [RS * t]

                def step(ins, wait=True):
                    ins.then_inc(r_step, 1)
                    n[0] = n[0] + 1
                    if wait:
                        dve.wait_ge(r_step, n[0])

                wait_apart(dve, regs, holds, (h_mm, t + 1), *([(hc_out, t)] if from_first(t) else []))
                step(dve.max(rval[:, :], h_ps[:, P:HW]), False)
                wait_apart(dve, regs, holds, (r_step, n[0]))
                step(dve.max_index(ridx[:, :], rval[:, :], h_ps[:, P:HW]), False)
                step(dve.tensor_scalar(rneg[:, :], rval[:, 0:1], -1.0, None, ALU.mult), True)
                step(dve.tensor_copy(ridx_f[:, :], ridx[:, 0:2]), False)
                dve.wait_ge(rexp_out, t + 1)
                step(dve.reciprocal(rinv[:, :], rsum[:, :]))
                step(dve.tensor_scalar(rp[:, :], rex[:, :], rinv[:, :], LORA_SCALE, ALU.mult, ALU.mult))
                step(dve.tensor_scalar(comb[:, 0, :], iota8, ridx_f[:, 0:1], rp[:, 0:1], ALU.is_equal, ALU.mult),
                     False)
                step(dve.tensor_scalar(comb[:, 1, :], iota8, ridx_f[:, 1:2], rp[:, 1:2], ALU.is_equal, ALU.mult))
                step(dve.tensor_tensor(combine[:, :], comb[:, 0, :], comb[:, 1, :], ALU.add))
                if from_first(t):
                    dve.wait_ge(ht_mm, t)
                dve.tensor_tensor(hc[:, :].rearrange("p (e r) -> p e r", e=E),
                                  h_ps[:, 0:P].rearrange("p (e r) -> p e r", e=E),
                                  combine[:, :].unsqueeze(2).broadcast_to([P, E, R]), ALU.mult
                                  ).then_inc(hc_out, 1)

            def bx_stacked(s):
                dve.wait_ge(bx_mm, s + 1)
                dve.tensor_tensor(bx[:, :], bx_ps, mask, ALU.mult).then_inc(bx_step, 1)
                dve.wait_ge(bx_step, BXS * s + 1)
                dve.tensor_copy(bx_hi[:, :], bx[:, :]).then_inc(bx_step, 1)
                dve.wait_ge(bx_step, BXS * s + 2)
                if from_first(s):
                    dve.wait_ge(s_mm, s)
                dve.tensor_copy(bx_stack[:, 0:2 * TR].rearrange("p (a c) -> p a c", a=2),
                                bx_hi[:, :].bitcast(F32).unsqueeze(1).broadcast_to([P, 2, TR])).then_inc(bx_step, 1)
                dve.tensor_tensor(bx_stack[:, 2 * TR:], bx[:, :], bx_hi[:, :].bitcast(F32), ALU.subtract
                                  ).then_inc(bx_step, 1)

            def slot(s, u, i):
                t, last = s - LAG, s - 1
                ul = (u - 1) % U
                if has(last):
                    top_delays(last, ul % 2)
                if has(t):
                    router(t)
                if has(last):
                    weights(last)
                    add_y(last, ul)
                if has_attn(s):
                    bx_stacked(s)
                if has(t):
                    dve.wait_ge(ht_h, t + 1)
                    dve.tensor_tensor(ht_lo[:, :], ht_ps, ht_hi[:, :].bitcast(F32), ALU.subtract).then_inc(ht_l, 1)
                if has(last):
                    for n in range(NSEL):
                        add_rolled(last, ul, n)
                if has_attn(s):
                    dve.wait_ge(eo_h, s + 1)
                    dve.tensor_tensor(eo_lo[:, :, :].rearrange("p a r -> p (a r)"),
                                      eo[:, :, :].rearrange("p a r -> p (a r)"),
                                      eo_hi[:, :, :].bitcast(F32).rearrange("p a r -> p (a r)"),
                                      ALU.subtract).then_inc(eo_l, 1)
                if has(t):
                    ut = (u - LAG) % U
                    dve.wait_ge(out_mm, t + 1)
                    dve.wait_ge(biased, t + 1)
                    dve.tensor_tensor(row[ut][:, :], o_ps[:, :], row[ut][:, :], ALU.add).then_inc(out_add, 1)
                if has(last):
                    for h in range(2):
                        dve.wait_ge(x2_h, 2 * last + 1 + h)
                        dve.tensor_tensor(x2_lo[:, 4 * h:4 * h + 4, :].rearrange("p k r -> p (k r)"),
                                          x_ps[:, h * 512:(h + 1) * 512],
                                          x2_hi[:, 4 * h:4 * h + 4, :].bitcast(F32).rearrange("p k r -> p (k r)"),
                                          ALU.subtract).then_inc(x2_l, 1)

            slots(dve, slot)

        @blk.gpsimd
        def _(pool):
            regs = [pool.alloc_register(f"pool_wait{n}") for n in range(3)]
            for u in range(U):
                pool.memset(mix[u][:, :], 0.0)
            pool.memset(eo[:, 4, :], 0.0).then_inc(cleared, 1)

            def bias_added(t, u):
                pool.wait_ge(x2_mm, 2 * t + 2)
                pool.tensor_tensor(row[u][:, :], row[u][:, :], bias[:, :], ALU.add).then_inc(biased, 1)

            def gather(s, u, i):
                wait_apart(pool, regs, holds, (top_step, TOPS * s + 10), (y_saved[u % 2], 32 * uses(s, u, i, 2)),
                           *([(sum_step, SUMS * s)] if from_first(s) else []))
                for n in range(NSEL):
                    pool.indirect_dma_start(out=rolled[n][:, :], out_offset=None, in_=y2_d[u],
                                            in_offset=bass.IndirectOffsetOnAxis(ap=off[:, n:n + 1], axis=0)
                                            ).then_inc(rolled_in[n], 16)

            def powers(s):
                n = [FS * s]

                def step(ins, wait=True):
                    ins.then_inc(fold_step, 1)
                    n[0] = n[0] + 1
                    if wait:
                        wait_apart(pool, regs, holds, (fold_step, n[0]))

                pool.wait_ge(sq_out, s + 1)
                if from_first(s):
                    pool.wait_ge(eo_h, s)
                    pool.wait_ge(eo_l, s)
                step(pool.tensor_tensor(eo[0:1, 4, :], sq[0:1, 0, 1, 0, :], sq[0:1, 0, 1, 1, :], ALU.add))
                step(pool.memset(sq[0:1, 0, 1, :, :], 0.0))
                step(pool.tensor_tensor(pw[:, 0, :], sq[:, 0, 0, :, :].rearrange("p h r -> p (h r)"),
                                        sq[:, 0, 1, :, :].rearrange("p h r -> p (h r)"), ALU.add), False)
                step(pool.tensor_tensor(pw[:, 1, :], sq[:, 1, 0, :, :].rearrange("p h r -> p (h r)"),
                                        sq[:, 1, 1, :, :].rearrange("p h r -> p (h r)"), ALU.add))
                step(pool.tensor_tensor(eo[:, 0:2, :], pw[:, :, 0:P], pw[:, :, P:2 * P], ALU.add), False)
                step(pool.tensor_tensor(eo[:, 2:4, :], pw[:, :, 0:P], pw[:, :, P:2 * P], ALU.subtract))

            def slot(s, u, i):
                t, last = s - LAG, s - 1
                if has(t):
                    bias_added(t, (u - LAG) % U)
                if has(last):
                    gather(last, *before(u, i, 1))
                if has_attn(s):
                    powers(s)

            slots(pool, slot)


_INS = ["x", "itok_B_4_50", "itok_B_0_15", "L0_cond_A", "L0_cond_B", "L0_cond2_weights", "L0_ffn_W_base",
        "L0_ffn_b_base", "L0_ffn_W_router", "L0_ffn_A_stack", "L0_ffn_B_stack"]


def kernel(**inputs):
    import concourse.bacc as bacc
    from concourse.bass_utils import run_bass_kernel_spmd as run

    nc = bacc.Bacc("TRN2", target_bir_lowering=False, num_devices=1)
    arrays = {f"in_{name}": np.ascontiguousarray(inputs[name]) for name in _INS}
    arrays.update({f"const_{name}": a for name, a in constants().items()})
    args = [nc.dram_tensor(name, a.shape, mybir.dt.from_np(a.dtype), kind="ExternalInput").ap()
            for name, a in arrays.items()]
    args.append(nc.dram_tensor("out", (NS, C, L), F32, kind="ExternalOutput").ap())
    build(nc, *args)
    return run(nc, [arrays], core_ids=[0]).results[0]["out"]
```

```python
from contextlib import ExitStack

import concourse.bass as bass
import numpy as np
from concourse import mybir

F32 = mybir.dt.float32
F32R = mybir.dt.float32r
I32 = mybir.dt.int32
U32 = mybir.dt.uint32
ALU = mybir.AluOpType
ACT = mybir.ActivationFunctionType

P = 128
NS, C, L = 64, 64, 1024
R = 16
E = 8
NT = NS * C // P
SPT = P // C
GS = P // R
NG = NS // GS
TPG = NT // NG
KC = L // P
Q = L // 4
H = L // 2
TR = SPT * R
STK = 3 * TR
HW = E * R + E
NCE = Q + 2
LAG = 2
U = 4
RB = 3
NSEL = 5
LORA_SCALE = 2.0

TALL = P + 1 + E
SMALL = TALL + P + STK
DCOLS = 2 * NCE + 6 * Q + NCE


def constants():
    def cos(n):
        return np.cos(2 * np.pi * (n % L) / L)

    def sin(n):
        s = np.sin(2 * np.pi * (n % L) / L)
        return np.where(n % H == 0, 0.0, s)

    i = np.arange(P)
    even = np.concatenate([2 * i, H - 2 * i])
    odd = np.concatenate([2 * i + 1, H - 1 - 2 * i])
    l = np.arange(Q)[:, None]
    ce = np.zeros((Q, NCE))
    ce[:, :Q] = cos(l * even)
    ce[:, Q] = cos(l[:, 0] * Q)
    se = sin(l * even)
    se[:, P] = sin(l[:, 0] * Q)
    se[0] = 0.0
    co = cos(l * odd)
    so = sin(l * odd)
    so[0] = sin(Q * odd)
    mid = np.zeros((P, NCE))
    mid[0, :Q] = np.rint(cos(Q * even))
    mid[0, Q] = 1.0

    def chunks(m):
        return [m[:P], m[P:]]

    dft = np.concatenate([*chunks(ce), *chunks(se), *chunks(co), *chunks(so), mid], axis=1)
    c = np.arange(Q)
    wt = np.full((P, 1), 2.0 / L)
    w0 = wt.copy()
    w0[0] = 1.0 / L
    fe, fo = 2 * i[:, None], 2 * i[:, None] + 1
    d_odd, d_even = 2 * c + 1, 2 * c + 2
    q = np.zeros((P, Q))
    q[0] = 2.0 / L * np.rint(cos(Q * d_even))
    back = np.concatenate([w0 * cos(fe * d_even), wt * cos(fo * d_even),
                           w0 * cos(fe * d_odd), wt * cos(fo * d_odd), q], axis=1)
    small = np.zeros((P, SMALL))
    small[:, :P] = np.eye(P)
    small[:, P] = np.arange(P) * 2 * L + 1
    small[:, P + 1:TALL] = np.arange(E)
    small[:TR, TALL:TALL + P] = (np.arange(TR)[:, None] // R) == (np.arange(P)[None, :] // C)
    small[:TR, TALL + P:] = np.tile(np.eye(TR), 3)
    return {"dft": dft.astype(np.float32), "back": back.astype(np.float32),
            "small": small.astype(np.float32)}


def build(nc, x, attn_ids, mix_ids, ad_a, ad_b, mix_w, w_base, b_base, w_router, a_stack, b_stack,
          dft, back, small, out):
    with ExitStack() as ctx:
        def sb(name, shape, dt=F32):
            return ctx.enter_context(nc.sbuf_tensor(name, shape, dt))

        y2_d = [nc.dram_tensor(f"y2_d{u}", (P * 2 * L, 1), F32, kind="Internal").ap() for u in range(U)]

        const = sb("const", [P, SMALL])
        ident = const[:, 0:P]
        rowbase = const[:, P:P + 1]
        iota8 = const[:, P + 1:TALL]
        mask = const[0:TR, TALL:TALL + P]
        repeat = const[0:TR, TALL + P:SMALL]
        ids = const[TR:TR + 1, TALL:TALL + 2 * NS].bitcast(I32)
        wt_hi = sb("wt_hi", [P, KC, L], F32R)
        wt_lo = sb("wt_lo", [P, KC, L], F32R)
        aw = sb("aw", [P, KC, HW])
        bs_hi = sb("bs_hi", [P, L], F32R)
        bs_lo = sb("bs_lo", [P, L], F32R)
        back_hi = sb("back_hi", [P, 5, Q], F32R)
        back_lo = sb("back_lo", [P, 4, Q], F32R)
        bias = sb("bias", [P, L])
        dft_m = sb("dft_m", [P, DCOLS])
        tiles(nc, locals())


def wait_apart(eng, regs, holds, *waits):
    if all(isinstance(value, int) for _, value in waits):
        regs = []
    else:
        for reg, (_, value) in zip(regs, waits):
            eng.reg_mov(reg, value)
        eng.wait_ge(*holds)
    for n, (sem, value) in enumerate(waits):
        eng.wait_ge(sem, regs[n] if regs else value)


def tiles(nc, v):
    x, out, y2_d = v["x"], v["out"], v["y2_d"]
    ident, mask, repeat, rowbase, iota8 = v["ident"], v["mask"], v["repeat"], v["rowbase"], v["iota8"]
    ids, bias, dft_m = v["ids"], v["bias"], v["dft_m"]
    wt_hi, wt_lo, aw = v["wt_hi"], v["wt_lo"], v["aw"]
    bs_hi, bs_lo, back_hi, back_lo = v["bs_hi"], v["bs_lo"], v["back_hi"], v["back_lo"]
    with ExitStack() as ctx:
        def sb(name, shape, dt=F32):
            return ctx.enter_context(nc.sbuf_tensor(name, shape, dt))

        def ps(name, cols):
            return ctx.enter_context(nc.psum_tensor(name, [P, cols], F32))

        def sem(name):
            return ctx.enter_context(nc.semaphore(name))

        row = [sb(f"row{u}", [P, L]) for u in range(U)]
        adapter = [sb(f"adapter{k}", [STK, 2 * L], F32R) for k in range(2)]
        mix = [sb(f"mix{u}", [P, P]) for u in range(U)]
        turn = sb("turn", [P, L])
        xt = turn[:, :].rearrange("p (k c) -> p k c", k=KC)
        x2 = turn[:, :].rearrange("p (k r) -> p k r", k=KC)
        sq = turn[:, :].rearrange("p (a b h r) -> p a b h r", a=2, b=2, h=2)
        pw = [turn[:, a * 2 * 2 * P:a * 2 * 2 * P + 2 * P] for a in range(2)]
        s_t = sb("s_t", [STK, P], F32R)
        eo = sb("eo", [P, 5, P])
        bx = eo[0:TR, 0, :]
        hc = eo[:, 1, :]
        eo_hi = sb("eo_hi", [P, 5, P], F32R)
        eo_lo = sb("eo_lo", [P, 5, P], F32R)
        y = sb("y", [P, L])
        corr0 = [sb(f"corr0_{k}", [P, 1]) for k in range(2)]
        rolled = [sb(f"rolled{n}", [P, L]) for n in range(RB)]
        val = sb("val", [P, 8])
        idx = sb("idx", [P, 8], U32)
        is_mid = sb("is_mid", [P, 2])
        not_mid = sb("not_mid", [P, 2])
        part = sb("part", [P, 2])
        in_even = sb("in_even", [P, 3])
        delay = sb("delay", [P, NSEL])
        mirror = sb("mirror", [P, 3])
        off = sb("off", [P, NSEL], U32)
        neg_max = sb("neg_max", [P, 1])
        ex = sb("ex", [P, NSEL + 1])
        ex_sum = sb("ex_sum", [P, 1])
        ex_inv = sb("ex_inv", [P, 1])
        weight = sb("weight", [P, NSEL + 1])
        rval = sb("rval", [P, 8])
        ridx = sb("ridx", [P, 8], U32)
        ridx_f = sb("ridx_f", [P, 2])
        rneg = sb("rneg", [P, 1])
        rex = sb("rex", [P, 2])
        rsum = sb("rsum", [P, 1])
        rinv = sb("rinv", [P, 1])
        rp = sb("rp", [P, 2])
        comb = sb("comb", [P, 2, E])
        combine = sb("combine", [P, E])
        ht_hi = sb("ht_hi", [P, P], F32R)
        ht_lo = sb("ht_lo", [P, P], F32R)
        x2_hi = sb("x2_hi", [P, KC, P], F32R)
        x2_lo = sb("x2_lo", [P, KC, P], F32R)
        r1 = sb("r1", [P, L])
        a_raw = r1[:, :].rearrange("p (s j r) -> p s j r", s=GS, j=KC)
        at = r1
        r2 = sb("r2", [P, 2 * (H + 1)])
        a_perm = r2[:, 0:L].rearrange("p (j c) -> p j c", j=KC)
        fold1 = r2[:, :].rearrange("p (a l) -> p a l", a=2)
        r3 = sb("r3", [P, L])
        fold2 = r3[:, :].rearrange("p (a l) -> p a l", a=4)
        b_raw = r3
        ft = sb("ft", [P, KC, P])
        bt = sb("bt", [P, KC, P])
        g_hi = sb("g_hi", [P, 2, L], F32R)
        g_lo = sb("g_lo", [P, 2, L], F32R)
        t_ps, x_ps, o_ps = ps("t_ps", L), ps("x_ps", L), ps("o_ps", L)
        h_ps, c_ps = ps("h_ps", 512), ps("c_ps", 512)
        ht_ps = h_ps[:, 256:256 + P]
        bx_ps = c_ps[0:TR, P:2 * P]
        s_ps = c_ps[0:STK, 0:P]

        small_in = sem("small_in")
        ids_in = sem("ids_in")
        dft_in = sem("dft_in")
        back_in = sem("back_in")
        st_in = sem("st_in")
        bias_in = sem("bias_in")
        w_in = [sem(f"w_in{n}") for n in range(RB)]
        a_in = sem("a_in")
        b_in = sem("b_in")
        row_in = [sem(f"row_in{u}") for u in range(U)]
        mix_in = [sem(f"mix_in{u}") for u in range(U)]
        adapter_in = [sem(f"adapter_in{k}") for k in range(2)]
        y_saved = sem("y_saved")
        rolled_in = [sem(f"rolled_in{n}") for n in range(RB)]
        out_saved = [sem(f"out_saved{u}") for u in range(U)]
        bst_side = sem("bst_side")
        st_ps = sem("st_ps")
        st_out = sem("st_out")
        bs_l = sem("bs_l")
        back_h = sem("back_h")
        back_l = sem("back_l")
        w_ps = sem("w_ps")
        w_h = sem("w_h")
        w_l = sem("w_l")
        a_side = sem("a_side")
        at_ps = sem("at_ps")
        at_out = sem("at_out")
        f1 = sem("f1")
        f2 = sem("f2")
        ft_ps = sem("ft_ps")
        ft_out = sem("ft_out")
        sp_ps = sem("sp_ps")
        g_h = sem("g_h")
        g_lo_at = sem("g_lo_at")
        g_lo_sp = sem("g_lo_sp")
        bt_ps = sem("bt_ps")
        bt_out = sem("bt_out")
        xt_ps = sem("xt_ps")
        bx_mm = sem("bx_mm")
        s_mm = sem("s_mm")
        spec_mm = sem("spec_mm")
        y_mm = sem("y_mm")
        corr_mm = sem("corr_mm")
        x2_mm = sem("x2_mm")
        h_mm = sem("h_mm")
        ht_mm = sem("ht_mm")
        out_mm = sem("out_mm")
        xt_out = sem("xt_out")
        s_hi = sem("s_hi")
        sq_out = sem("sq_out")
        y_out = sem("y_out")
        y_free = sem("y_free")
        eo_h = sem("eo_h")
        exp_out = sem("exp_out")
        rexp_out = sem("rexp_out")
        ht_h = sem("ht_h")
        x2_f = sem("x2_f")
        x2_h = sem("x2_h")
        bx_out = sem("bx_out")
        s_lo = sem("s_lo")
        eo_l = sem("eo_l")
        top_step = sem("top_step")
        w_step = sem("w_step")
        sum_step = sem("sum_step")
        r_step = sem("r_step")
        hc_out = sem("hc_out")
        ht_l = sem("ht_l")
        x2_l = sem("x2_l")
        out_add = sem("out_add")
        cleared = sem("cleared")
        biased = sem("biased")
        fold_step = sem("fold_step")
        blk = ctx.enter_context(nc.Block())
        TOPS, RS, FS = 15, 9, 6
        SUMS = NSEL + 1
        holds = (cleared, 1)

        a_st, r_st = row[3], row[1]
        b_st = row[2][:, :].rearrange("p (e j r) -> p e j r", e=E, j=KC)

        def slots(eng, slot):
            for s in range(U):
                slot(s, s % U, s // U)
            with eng.Fori(1, NG - 1) as i:
                for u in range(U):
                    slot(i * U + u, u, i)
            for s in range(NT - U, NT + LAG):
                slot(s, s % U, s // U)

        def has_attn(s):
            return not isinstance(s, int) or s < NT

        def has(t):
            return not isinstance(t, int) or 0 <= t < NT

        def from_first(t):
            return not isinstance(t, int) or t > 0

        def has_group(g):
            return not isinstance(g, int) or g < NG

        def before(u, i, n):
            return ((u - n) % U, i + (u - n) // U)

        def adapter_loads(u, i):
            return (i * (U // 2) + u // 2 + 1) * 48

        def load_w(eng, m):
            if m >= RB:
                eng.wait_ge(w_ps, m - RB + 1)
            eng.dma_start(rolled[m % RB][:, :], v["w_base"].rearrange("(m p) i -> m p i", p=P)[m]
                          ).then_inc(w_in[m % RB], 16)

        def w_at(m):
            return t_ps if m in (0, 2, 3) else o_ps

        def first(s):
            return isinstance(s, int) and s == 0

        @blk.sync
        def _(sp):
            regs = [sp.alloc_register(f"sp_wait{n}") for n in range(3)]
            x_t = x.rearrange("(t b) c l -> t (b c) l", b=SPT)
            out_t = out.rearrange("(t b) c l -> t (b c) l", b=SPT)
            a_src = v["ad_a"].rearrange("n (p j) r -> n p (j r)", p=P)
            a_dst = r1[:, :].rearrange("p (s f) -> p s f", s=GS)

            def sample_id(n, most):
                return sp.value_load(ids[0:1, bass.ds(n, 1)], min_val=0, max_val=most)

            def load_a(g):
                for s in range(GS):
                    n = sample_id(g * GS + s, NS - 1)
                    if s == 0 and from_first(g):
                        wait_apart(sp, regs, holds, (g_h, 2 * g), (g_lo_at, g), (f1, 3 * g))
                    sp.dma_start(a_dst[:, s, :], a_src[bass.ds(n, 1)].rearrange("o p f -> (o p) f")
                                 ).then_inc(a_in, 16)

            def load_b(g, dst=b_raw):
                for s in range(GS):
                    n = sample_id(g * GS + s, NS - 1)
                    if s == 0 and from_first(g):
                        sp.wait_ge(ft_ps, g + 1)
                    sp.dma_start(dst[s * R:(s + 1) * R, :],
                                 v["ad_b"][bass.ds(n, 1)].rearrange("o r l -> (o r) l")).then_inc(b_in, 16)

            def load_row(t, u, i):
                if not isinstance(t, int) or t >= U:
                    sp.wait_ge(out_saved[u], i * 16)
                elif t == 1:
                    sp.wait_ge(st_ps, 2)
                elif t == 2:
                    sp.wait_ge(bt_ps, 1)
                sp.dma_start(row[u][:, :], x_t[bass.ds(t, 1)].rearrange("o p l -> (o p) l")
                             ).then_inc(row_in[u], 16)

            def load_adapter(t, u, i):
                if u == 0:
                    wait_apart(sp, regs, holds, (g_h, 2 * i + 2), (g_lo_at, i + 1), (g_lo_sp, i + 1))
                if not isinstance(t, int) or t >= 2:
                    sp.wait_ge(y_mm, t - 1)
                k = u % 2
                for n, src in enumerate((g_hi, g_lo, g_hi)):
                    sp.dma_start(adapter[k][n * TR:(n + 1) * TR, :].bitcast(F32),
                                 src[u * TR:(u + 1) * TR, :, :].bitcast(F32).rearrange("p a l -> p (a l)")
                                 ).then_inc(adapter_in[k], 16)

            def load_mix(t, u):
                for b in range(SPT):
                    n = sample_id(t * SPT + b + NS, v["mix_w"].shape[0] - 1)
                    sp.dma_start(mix[u][b * C:(b + 1) * C, b * C:(b + 1) * C],
                                 v["mix_w"][bass.ds(n, 1)].rearrange("o c d -> (o c) d")
                                 ).then_inc(mix_in[u], 16)

            def slot(s, u, i):
                un, in_ = (u + 1) % U, i + (u + 1) // U
                if has_attn(s + 1):
                    load_adapter(s + 1, un, in_)
                    load_row(s + 1, un, in_)
                    load_mix(s + 1, un)
                if u == 3 and has_group(i + 2):
                    load_a(i + 2)
                if u == 1 and has_group(i + 1):
                    load_b(i + 1)
                t = s - LAG
                if has(t):
                    ut, it = before(u, i, LAG)
                    sp.wait_ge(out_add, t + 1)
                    sp.dma_start(out_t[bass.ds(t, 1)].rearrange("o p l -> (o p) l"), row[ut][:, :]
                                 ).then_inc(out_saved[ut], 16)

            sp.dma_start(ids[0:1, 0:NS], v["attn_ids"].rearrange("(o n) -> o n", o=1)).then_inc(ids_in, 16)
            sp.dma_start(ids[0:1, NS:2 * NS], v["mix_ids"].rearrange("(o n) -> o n", o=1)).then_inc(ids_in, 16)
            sp.wait_ge(ids_in, 32)
            load_a(0)
            load_row(0, 0, 0)
            sp.wait_ge(bst_side, 1)
            load_b(0, row[2])
            for m in range(RB, KC - 2):
                load_w(sp, m)
            sp.wait_ge(cleared, 1)
            load_mix(0, 0)
            load_adapter(0, 0, 0)
            for m in range(KC - 2, KC):
                load_w(sp, m)
            load_a(1)
            slots(sp, slot)
            for u in range(U):
                sp.wait_ge(out_saved[u], 16 * NT // U)

        @blk.tensor
        def _(pe):
            def three(dst, pairs, start, stop):
                n, last = 0, None
                todo = [(a, b) for (ah, al), (bh, bl) in pairs for a, b in ((ah, bh), (ah, bl), (al, bh))]
                for a, b in todo:
                    last = pe.matmul(dst, a, b, start=start and n == 0, stop=stop and n == len(todo) - 1)
                    n += 1
                return last

            def transposed(dst, chunks):
                for n, src in enumerate(chunks):
                    last = pe.transpose(dst[:, n * P:(n + 1) * P], src, ident)
                return last

            def a_transposed(g):
                pe.wait_ge(a_side, g + 1)
                transposed(x_ps, [a_perm[:, j, :] for j in range(KC)]).then_inc(at_ps, 1)

            def fold_transposed(g):
                pe.wait_ge(f2, 5 * g + 5)
                transposed(x_ps, [fold2[:, j // 2, (j % 2) * P:(j % 2 + 1) * P] for j in range(KC)]
                           ).then_inc(ft_ps, 1)

            def a_spectrum(g, odd):
                if not odd:
                    pe.wait_ge(ft_out, g + 1)

                def mm(dst, c, at0, width, start=False, stop=False):
                    return pe.matmul(dst, ft[:, c, :], dft_m[:, at0:at0 + width], start=start, stop=stop,
                                     skip_group_check=True)

                ev, od = x_ps[:, 0:512], x_ps[:, 512:1024]
                sines = 2 * NCE
                if not odd:
                    mm(ev[:, 0:NCE], 0, 0, NCE, start=True)
                    mm(ev[:, 0:NCE], 1, NCE, NCE)
                    mm(ev[:, 0:NCE], 4, DCOLS - NCE, NCE)
                    mm(ev[:, Q:2 * Q], 4, sines, Q)
                    mm(ev[:, Q:2 * Q], 5, sines + Q, Q, stop=True)
                    return
                mm(od[:, 0:Q], 2, sines + 2 * Q, Q, start=True)
                mm(od[:, 0:Q], 3, sines + 3 * Q, Q)
                mm(od[:, Q:2 * Q], 6, sines + 4 * Q, Q)
                mm(od[:, Q:2 * Q], 7, sines + 5 * Q, Q, stop=True).then_inc(sp_ps, 1)

            def b_transposed(g, src=b_raw, dst=x_ps):
                pe.wait_ge(b_in, (g + 1) * 16 * GS)
                transposed(dst, [src[:, j * P:(j + 1) * P] for j in range(KC)]).then_inc(bt_ps, 1)

            def x_transposed(s, u, i, half):
                if half == 0:
                    pe.wait_ge(row_in[u], (i + 1) * 16)
                    if from_first(s):
                        pe.wait_ge(y_free, s)
                for c in range(4 * half, 4 * half + 4):
                    last = pe.transpose(t_ps[:, c * P:(c + 1) * P], row[u][:, c * P:(c + 1) * P], ident)
                last.then_inc(xt_ps, 1)

            def b_times_x(s, u, i):
                if u == 0:
                    pe.wait_ge(bt_out, i + 1)
                if from_first(s):
                    pe.wait_ge(top_step, TOPS * (s - 1) + 2)
                for c in range(KC):
                    if c % 4 == 0:
                        pe.wait_ge(xt_out, 2 * s + 1 + c // 4)
                    last = pe.matmul(bx_ps, bt[:, c, u * TR:(u + 1) * TR], xt[:, c, :],
                                     start=c == 0, stop=c == KC - 1)
                last.then_inc(bx_mm, 1)

            def bx_repeated(s):
                pe.wait_ge(bx_out, s + 1)
                pe.matmul(s_ps, repeat, bx, start=True, stop=True).then_inc(s_mm, 1)

            def spectrum(s, u, i):
                pe.wait_ge(adapter_in[u % 2], adapter_loads(u, i))
                pe.wait_ge(s_lo, s + 1)
                pe.wait_ge(xt_out, 2 * s + 2)
                for c in range(KC):
                    last = pe.matmul(t_ps[:, c * P:(c + 1) * P], adapter[u % 2][:, L + c * P:L + (c + 1) * P],
                                     s_t[:, :], start=True, stop=True)
                last.then_inc(spec_mm, 1)

            def adapter_out(s, u):
                pe.wait_ge(sq_out, s + 1)
                for h in range(2):
                    last = pe.matmul(t_ps[:, h * 512:(h + 1) * 512], s_t[:, :],
                                     adapter[u % 2][:, h * 512:(h + 1) * 512], start=True, stop=True)
                last.then_inc(y_mm, 1)

            def correlation(s):
                pe.wait_ge(eo_h, s + 1)
                pe.wait_ge(eo_l, s + 1)

                def pair(n):
                    return (eo_hi[:, n, :], eo_lo[:, n, :]), (back_hi[:, n, :], back_lo[:, n, :])
                three(c_ps[:, 0:Q], [pair(2), pair(3)], True, True)
                three(c_ps[:, Q:2 * Q], [pair(0), pair(1)], True, False)
                pe.matmul(c_ps[:, Q:2 * Q], eo_hi[:, 4, :], back_hi[:, 4, :], start=False, stop=False)
                pe.matmul(c_ps[:, Q:2 * Q], eo_lo[:, 4, :], back_hi[:, 4, :], start=False, stop=True
                          ).then_inc(corr_mm, 1)

            def mixed(t, u, i):
                pe.wait_ge(mix_in[u], (i + 1) * 32)
                pe.wait_ge(sum_step, SUMS * t + SUMS)
                for c in range(KC):
                    last = pe.matmul(x_ps[:, c * P:(c + 1) * P], row[u][:, c * P:(c + 1) * P], mix[u][:, :],
                                     start=True, stop=True)
                    if c % 4 == 3:
                        last.then_inc(x2_mm, 1)

            def project(t):
                if from_first(t):
                    pe.wait_ge(ht_l, t)
                for c in range(KC):
                    if c % 4 == 0:
                        pe.wait_ge(x2_f, 2 * t + 1 + c // 4)
                    last = pe.matmul(h_ps[:, 0:HW], x2[:, c, :], aw[:, c, :], start=c == 0, stop=c == KC - 1)
                last.then_inc(h_mm, 1)

            def h_transposed(t):
                pe.wait_ge(hc_out, t + 1)
                pe.transpose(ht_ps, hc, ident).then_inc(ht_mm, 1)

            def base(t, c):
                if c % 4 == 0:
                    pe.wait_ge(x2_l, 2 * t + 1 + c // 4)
                if c == 0 and from_first(t):
                    pe.wait_ge(out_add, t)
                for h in range(2):
                    cols = slice(h * 512, (h + 1) * 512)
                    three(o_ps[:, cols], [((x2_hi[:, c, :], x2_lo[:, c, :]),
                                           (wt_hi[:, c, cols], wt_lo[:, c, cols]))], c == 0, False)

            def experts(t):
                pe.wait_ge(ht_l, t + 1)
                for h in range(2):
                    cols = slice(h * 512, (h + 1) * 512)
                    last = three(o_ps[:, cols], [((ht_hi[:, :], ht_lo[:, :]), (bs_hi[:, cols], bs_lo[:, cols]))],
                                 False, True)
                last.then_inc(out_mm, 1)

            def w_transposed(m):
                pe.wait_ge(w_in[m % RB], 16 * (m // RB + 1))
                pe.wait_ge(*((st_out, 1), (bs_l, 1), (w_l, 1), (w_l, 3), (bt_out, 1), (w_l, 5), (w_l, 6),
                             (w_l, 7))[m])
                transposed(w_at(m), [rolled[m % RB][:, j * P:(j + 1) * P] for j in range(KC)]).then_inc(w_ps, 1)

            def slot(s, u, i):
                t, g = s - LAG, i + 1
                attn, ffn, prep = has_attn(s), has(t), has_group(g)
                if ffn:
                    project(t)
                for c in range(KC):
                    if ffn:
                        base(t, c)
                    if c < 2 and attn and not first(s):
                        x_transposed(s, u, i, c)
                    if c == 2 and attn and not first(s):
                        b_times_x(s, u, i)
                    if c == 2 and u in (0, 2) and prep and ffn:
                        pe.wait_ge(x2_l, 2 * t + 2)
                    if c == (6 if first(s) else 2) and u == 0 and prep:
                        a_transposed(g)
                    if c == 3 and ffn:
                        h_transposed(t)
                    if c == 3 and attn and not first(s):
                        bx_repeated(s)
                    if c == 3 and u == 2 and prep:
                        a_spectrum(g, False)
                    if c == 4 and attn:
                        spectrum(s, u, i)
                    if c == 4 and u == 2 and prep:
                        a_spectrum(g, True)
                    if c == 4 and u == 3 and prep:
                        b_transposed(g)
                    if c == 6 and u == 1 and prep:
                        fold_transposed(g)
                    if c == 5 and attn:
                        adapter_out(s, u)
                    if first(s) and c in (4, 5):
                        w_transposed(KC - 6 + c)
                if ffn:
                    experts(t)
                if has(s - 1):
                    if prep and u == 0:
                        pe.wait_ge(at_out, 2 * g + 2)
                    if prep and u == 1:
                        pe.wait_ge(ft_out, g + 1)
                    if prep and u == 2:
                        pe.wait_ge(g_h, 2 * g + 2)
                        pe.wait_ge(g_lo_sp, g + 1)
                    if prep and u == 3:
                        pe.wait_ge(bt_out, g + 1)
                    mixed(s - 1, *before(u, i, 1))
                if attn:
                    correlation(s)

            pe.wait_ge(small_in, 32)
            pe.wait_ge(st_in, 48)
            for k in range(KC):
                at0 = (k // 3) * 512 + (k % 3) * HW
                dst = t_ps[:, at0:at0 + HW] if k < 6 else c_ps[:, (k - 6) * HW:(k - 5) * HW]
                pe.transpose(dst[:, 0:P], a_st[:, k * P:(k + 1) * P], ident)
                last = pe.transpose(dst[:, P:HW], r_st[0:E, k * P:(k + 1) * P], ident[0:E, 0:E])
            last.then_inc(st_ps, 1)
            pe.wait_ge(bst_side, 1)
            transposed(o_ps, [a_perm[:, j, :] for j in range(KC)]).then_inc(st_ps, 1)

            w_transposed(0)
            a_transposed(0)
            w_transposed(1)
            w_transposed(2)
            fold_transposed(0)
            pe.wait_ge(w_l, 2)
            b_transposed(0, row[2], o_ps)
            w_transposed(3)
            pe.wait_ge(dft_in, 16)
            a_spectrum(0, False)
            a_spectrum(0, True)
            pe.wait_ge(w_l, 4)
            x_transposed(0, 0, 0, 0)
            x_transposed(0, 0, 0, 1)
            w_transposed(4)
            b_times_x(0, 0, 0)
            w_transposed(5)
            bx_repeated(0)
            pe.wait_ge(g_h, 2)
            pe.wait_ge(g_lo_sp, 1)
            slots(pe, slot)

        @blk.scalar
        def _(act):
            def copy(dst, src):
                return act.activation(dst, src, ACT.Copy)

            def flat(ap, rule):
                return ap.rearrange(rule)

            def side_by_side(src):
                return copy(a_perm.rearrange("p j (s r) -> p j s r", s=GS), src.rearrange("p s j r -> p j s r"))

            def a_beside(g):
                act.wait_ge(a_in, (g + 1) * 16 * GS)
                if from_first(g):
                    act.wait_ge(f2, 5 * g)
                else:
                    act.wait_ge(st_ps, 2)
                side_by_side(a_raw).then_inc(a_side, 1)

            def a_out(g):
                act.wait_ge(at_ps, g + 1)
                act.wait_ge(a_side, g + 1)
                for b in range(2):
                    copy(at[:, :].rearrange("q (p j) -> q j p", j=KC)[:, 4 * b:4 * b + 4, :],
                         x_ps[:, b * 512:(b + 1) * 512].rearrange("q (j p) -> q j p", j=4)).then_inc(at_out, 1)

            def fold_out(g):
                act.wait_ge(ft_ps, g + 1)
                copy(ft[:, :, :].rearrange("p k c -> p (k c)"), x_ps[:, :]).then_inc(ft_out, 1)

            def a_high(g, u, i):
                act.wait_ge(at_out, 2 * g + 2)
                if from_first(g):
                    act.wait_ge(adapter_in[(u + 1) % 2], adapter_loads(u + 1, i))
                copy(g_hi[:, 0, :], at[:, :]).then_inc(g_h, 1)

            def spectrum_high(g):
                act.wait_ge(sp_ps, g + 1)
                copy(g_hi[:, 1, :], x_ps[:, :]).then_inc(g_h, 1)

            def b_out(g, src=x_ps):
                act.wait_ge(bt_ps, g + 1)
                copy(bt[:, :, :].rearrange("p k c -> p (k c)"), src[:, :]).then_inc(bt_out, 1)

            def w_high(m):
                act.wait_ge(w_ps, m + 1)
                copy(wt_hi[:, :, m * P:(m + 1) * P],
                     w_at(m)[:, :].rearrange("p (k o) -> p k o", k=KC)).then_inc(w_h, 1)

            def x_out(s, t):
                for h in range(2):
                    act.wait_ge(xt_ps, 2 * s + 1 + h)
                    if h == 0 and has(t):
                        act.wait_ge(h_mm, t + 1)
                    elif h == 0 and isinstance(s, int) and s == 1:
                        act.wait_ge(fold_step, FS)
                    act.activation(xt[:, 4 * h:4 * h + 4, :].rearrange("p k c -> p (k c)"),
                                   t_ps[:, h * 512:(h + 1) * 512], ACT.Copy).then_inc(xt_out, 1)

            def stack_high(s):
                act.wait_ge(s_mm, s + 1)
                if from_first(s):
                    act.wait_ge(y_mm, s)
                act.activation(s_t[:, :], s_ps, ACT.Copy).then_inc(s_hi, 1)

            def slot(s, u, i):
                t, last, g = s - LAG, s - 1, i + 1
                attn, prep = has_attn(s), has_group(g)
                if has(last):
                    act.wait_ge(top_step, TOPS * last + TOPS)
                    if from_first(last):
                        act.wait_ge(w_step, 2 * last)
                    act.activation(ex[:, :], val[:, 0:NSEL + 1], ACT.Exp, bias=neg_max[:, :],
                                   accum_out=ex_sum[:, :]).then_inc(exp_out, 1)
                if has(t):
                    act.wait_ge(r_step, RS * t + 3)
                    act.activation(rex[:, :], rval[:, 0:2], ACT.Exp, bias=rneg[:, :],
                                   accum_out=rsum[:, :]).then_inc(rexp_out, 1)
                if attn and not first(s):
                    x_out(s, t)
                if prep and u == 0 and not first(s):
                    a_out(g)
                if has(t):
                    act.wait_ge(ht_mm, t + 1)
                    if from_first(t):
                        act.wait_ge(out_mm, t)
                    act.activation(ht_hi[:, :], ht_ps, ACT.Copy).then_inc(ht_h, 1)
                if attn and not first(s):
                    stack_high(s)
                if prep and u == 2:
                    a_high(g, u, i)
                if attn:
                    act.wait_ge(spec_mm, s + 1)
                    act.activation(turn[:, :], t_ps[:, :], ACT.Square).then_inc(sq_out, 1)
                if first(s):
                    w_high(KC - 2)
                if prep and u == 2:
                    spectrum_high(g)
                if prep and u == 3:
                    b_out(g)
                if attn:
                    act.wait_ge(y_mm, s + 1)
                    if from_first(s):
                        act.wait_ge(sum_step, SUMS * (s - 1) + 1)
                        act.wait_ge(y_saved, 32 * s)
                    act.activation(y[:, :], t_ps[:, :], ACT.Copy).then_inc(y_out, 1)
                    act.wait_ge(y_out, s + 1)
                    act.activation(t_ps[:, :], y[:, :], ACT.Square, accum_out=corr0[u % 2][:, :]).then_inc(y_free, 1)
                    y2 = y2_d[u].rearrange("(p l) o -> p (l o)", p=P)
                    for h in range(2):
                        act.dma_start(y2[:, h * L:(h + 1) * L], y[:, :]).then_inc(y_saved, 16)
                    act.wait_ge(fold_step, FS * s + FS)
                    if from_first(s):
                        act.wait_ge(corr_mm, s)
                        act.wait_ge(eo_l, s)
                    act.activation(eo_hi[:, :, :].rearrange("p a r -> p (a r)"),
                                   eo[:, :, :].rearrange("p a r -> p (a r)"), ACT.Copy).then_inc(eo_h, 1)
                if first(s):
                    w_high(KC - 1)
                    a_beside(1)
                    a_out(1)
                if prep and u == 1:
                    fold_out(g)
                if has(last):
                    for h in range(2):
                        act.wait_ge(x2_mm, 2 * last + 1 + h)
                        act.activation(x2[:, 4 * h:4 * h + 4, :].rearrange("p k r -> p (k r)"),
                                       x_ps[:, h * 512:(h + 1) * 512], ACT.Copy).then_inc(x2_f, 1)
                        act.activation(x2_hi[:, 4 * h:4 * h + 4, :].rearrange("p k r -> p (k r)"),
                                       x_ps[:, h * 512:(h + 1) * 512], ACT.Copy).then_inc(x2_h, 1)
                if u == 3 and has_group(g + 1):
                    a_beside(g + 1)

            act.dma_start(v["const"][:, 0:TALL], v["small"][:, 0:TALL]).then_inc(small_in, 16)
            act.dma_start(row[2][:, :].rearrange("p (e f) -> p e f", e=E),
                          v["b_stack"].rearrange("e (p j) r -> p e (j r)", p=P)).then_inc(st_in, 16)
            act.dma_start(a_st[:, :], v["a_stack"].rearrange("e r d -> (e r) d")).then_inc(st_in, 16)
            act.dma_start(r_st[0:E, :], v["w_router"]).then_inc(st_in, 16)
            act.dma_start(v["const"][0:TR, TALL:SMALL], v["small"][0:TR, TALL:SMALL]).then_inc(small_in, 16)
            load_w(act, 0)
            act.wait_ge(st_in, 48)
            side_by_side(b_st).then_inc(bst_side, 1)
            for m in range(1, RB):
                load_w(act, m)
            act.wait_ge(st_ps, 1)
            copy(aw[:, 0:3, :], t_ps[:, 0:3 * HW].rearrange("p (k c) -> p k c", k=3))
            copy(aw[:, 3:6, :], t_ps[:, 512:512 + 3 * HW].rearrange("p (k c) -> p k c", k=3)).then_inc(st_out, 1)
            copy(aw[:, 6:8, :], c_ps[:, 0:2 * HW].rearrange("p (k c) -> p k c", k=2)).then_inc(st_out, 1)
            act.wait_ge(st_ps, 2)
            copy(bs_hi[:, :].rearrange("q (p j) -> q j p", j=KC),
                 o_ps[:, :].rearrange("q (j p) -> q j p", j=KC)).then_inc(st_out, 1)
            a_beside(0)
            act.dma_start(dft_m[:, :], v["dft"]).then_inc(dft_in, 16)
            act.dma_start(y[:, :], v["back"][:, 0:4 * Q]).then_inc(back_in, 16)
            act.dma_start(turn[:, 0:Q], v["back"][:, 4 * Q:5 * Q]).then_inc(back_in, 16)
            act.dma_start(bias[:, :], v["b_base"].rearrange("(o n) -> o n", o=1).broadcast_to([P, L])
                          ).then_inc(bias_in, 16)
            w_high(0)
            a_out(0)
            w_high(1)
            w_high(2)
            a_high(0, 3, -1)
            act.wait_ge(back_in, 32)
            copy(back_hi[:, 0:4, :].rearrange("p a c -> p (a c)"), y[:, :]).then_inc(back_h, 1)
            copy(back_hi[:, 4, :], turn[:, 0:Q]).then_inc(back_h, 1)
            fold_out(0)
            b_out(0, o_ps)
            w_high(3)
            act.wait_ge(back_h, 2)
            x_out(0, -LAG)
            spectrum_high(0)
            w_high(4)
            stack_high(0)
            w_high(5)
            slots(act, slot)

        @blk.vector
        def _(dve):
            regs = [dve.alloc_register(f"dve_wait{n}") for n in range(2)]

            def low(dst, src, hi):
                return dve.tensor_tensor(dst, src, hi.bitcast(F32), ALU.subtract)

            def top_delays(s, k):
                n = [TOPS * s]

                def step(ins, wait=True):
                    ins.then_inc(top_step, 1)
                    n[0] = n[0] + 1
                    if wait:
                        dve.wait_ge(top_step, n[0])

                corr = c_ps[:, :]
                wait_apart(dve, regs, holds, (corr_mm, s + 1), *([(exp_out, s)] if from_first(s) else []))
                step(dve.max(val[:, :], corr), False)
                wait_apart(dve, regs, holds, (top_step, n[0]))
                step(dve.max_index(idx[:, :], val[:, :], corr))
                step(dve.tensor_scalar(in_even[:, :], idx[:, 0:3], float(Q), 1.0 - H, ALU.is_ge, ALU.mult))
                step(dve.scalar_tensor_tensor(delay[:, 0:3], idx[:, 0:3], 2.0, in_even[:, :], ALU.mult, ALU.add))
                step(dve.tensor_scalar(off[:, 0:3], delay[:, 0:3], rowbase, None, ALU.add), False)
                step(dve.tensor_scalar(is_mid[:, :], idx[:, 0:2], float(H - 1), None, ALU.is_equal), False)
                step(dve.tensor_scalar(not_mid[:, :], idx[:, 0:2], float(H - 1), None, ALU.not_equal), False)
                step(dve.tensor_scalar(mirror[:, :], delay[:, 0:3], -1.0, float(L - 2), ALU.mult, ALU.add))
                step(dve.tensor_tensor(part[:, :], mirror[:, 0:2], not_mid[:, :], ALU.mult))
                step(dve.scalar_tensor_tensor(delay[:, 3:5], is_mid[:, :], mirror[:, 2:3], part[:, :],
                                              ALU.mult, ALU.add))
                step(dve.tensor_scalar(off[:, 3:5], delay[:, 3:5], rowbase, None, ALU.add), False)
                step(dve.tensor_tensor(part[:, :], val[:, 0:2], not_mid[:, :], ALU.mult))
                dve.wait_ge(y_free, s + 1)
                step(dve.tensor_scalar(neg_max[:, :], val[:, 0:1], corr0[k][:, :], -1.0, ALU.max, ALU.mult), False)
                step(dve.scalar_tensor_tensor(val[:, 3:5], is_mid[:, :], val[:, 2:3], part[:, :],
                                              ALU.mult, ALU.add), False)
                step(dve.tensor_copy(val[:, 5:6], corr0[k][:, :]), False)

            def weights(s):
                dve.wait_ge(exp_out, s + 1)
                dve.reciprocal(ex_inv[:, :], ex_sum[:, :]).then_inc(w_step, 1)
                dve.wait_ge(w_step, 2 * s + 1)
                if from_first(s):
                    dve.wait_ge(sum_step, SUMS * s)
                dve.tensor_scalar(weight[:, :], ex[:, :], ex_inv[:, :], None, ALU.mult).then_inc(w_step, 1)
                dve.wait_ge(w_step, 2 * s + 2)

            def add_y(s, u):
                dve.scalar_tensor_tensor(row[u][:, :], y[:, :], weight[:, 5:6], row[u][:, :],
                                         ALU.mult, ALU.add).then_inc(sum_step, 1)

            def add_rolled(s, u, n):
                a_tile = (NSEL - 1 - n % RB) // RB + 1
                dve.wait_ge(rolled_in[n % RB], 16 * (a_tile * s + n // RB + 1))
                dve.wait_ge(sum_step, SUMS * s + n + 1)
                dve.scalar_tensor_tensor(row[u][:, :], rolled[n % RB][:, :], weight[:, n:n + 1], row[u][:, :],
                                         ALU.mult, ALU.add).then_inc(sum_step, 1)

            def router(t):
                n = [RS * t]

                def step(ins, wait=True):
                    ins.then_inc(r_step, 1)
                    n[0] = n[0] + 1
                    if wait:
                        dve.wait_ge(r_step, n[0])

                wait_apart(dve, regs, holds, (h_mm, t + 1), *([(hc_out, t)] if from_first(t) else []))
                step(dve.max(rval[:, :], h_ps[:, P:HW]), False)
                wait_apart(dve, regs, holds, (r_step, n[0]))
                step(dve.max_index(ridx[:, :], rval[:, :], h_ps[:, P:HW]), False)
                step(dve.tensor_scalar(rneg[:, :], rval[:, 0:1], -1.0, None, ALU.mult), True)
                step(dve.tensor_copy(ridx_f[:, :], ridx[:, 0:2]), False)
                dve.wait_ge(rexp_out, t + 1)
                step(dve.reciprocal(rinv[:, :], rsum[:, :]))
                step(dve.tensor_scalar(rp[:, :], rex[:, :], rinv[:, :], LORA_SCALE, ALU.mult, ALU.mult))
                step(dve.tensor_scalar(comb[:, 0, :], iota8, ridx_f[:, 0:1], rp[:, 0:1], ALU.is_equal, ALU.mult),
                     False)
                step(dve.tensor_scalar(comb[:, 1, :], iota8, ridx_f[:, 1:2], rp[:, 1:2], ALU.is_equal, ALU.mult))
                step(dve.tensor_tensor(combine[:, :], comb[:, 0, :], comb[:, 1, :], ALU.add))
                dve.tensor_tensor(hc.rearrange("p (e r) -> p e r", e=E),
                                  h_ps[:, 0:P].rearrange("p (e r) -> p e r", e=E),
                                  combine[:, :].unsqueeze(2).broadcast_to([P, E, R]), ALU.mult
                                  ).then_inc(hc_out, 1)

            def bx_masked(s):
                dve.wait_ge(bx_mm, s + 1)
                dve.tensor_tensor(bx, bx_ps, mask, ALU.mult).then_inc(bx_out, 1)

            def stack_low(s):
                dve.wait_ge(s_hi, s + 1)
                low(s_t[2 * TR:STK, :], s_ps[2 * TR:STK, :], s_t[2 * TR:STK, :]).then_inc(s_lo, 1)

            def spectrum_low(g):
                dve.wait_ge(g_h, 2 * g + 2)
                low(g_lo[:, 1, :], x_ps[:, :], g_hi[:, 1, :]).then_inc(g_lo_sp, 1)

            def w_low(m):
                dve.wait_ge(w_h, m + 1)
                low(wt_lo[:, :, m * P:(m + 1) * P],
                    w_at(m)[:, :].rearrange("p (k o) -> p k o", k=KC),
                    wt_hi[:, :, m * P:(m + 1) * P]).then_inc(w_l, 1)

            def slot(s, u, i):
                t, last, g = s - LAG, s - 1, i + 1
                ul = (u - 1) % U
                if has(last):
                    top_delays(last, ul % 2)
                if has(t):
                    router(t)
                if has(last):
                    weights(last)
                    add_y(last, ul)
                if has_attn(s) and not first(s):
                    bx_masked(s)
                if has(last):
                    add_rolled(last, ul, 0)
                if has(t):
                    dve.wait_ge(ht_h, t + 1)
                    low(ht_lo[:, :], ht_ps, ht_hi[:, :]).then_inc(ht_l, 1)
                if has_attn(s) and not first(s):
                    stack_low(s)
                if first(s):
                    w_low(KC - 2)
                    w_low(KC - 1)
                if has(last):
                    for n in range(1, NSEL):
                        if n == 2 and u == 2 and has_group(g):
                            spectrum_low(g)
                        add_rolled(last, ul, n)
                if has_attn(s):
                    dve.wait_ge(eo_h, s + 1)
                    low(eo_lo[:, :, :].rearrange("p a r -> p (a r)"), eo[:, :, :].rearrange("p a r -> p (a r)"),
                        eo_hi[:, :, :].rearrange("p a r -> p (a r)")).then_inc(eo_l, 1)
                if has(t):
                    ut = (u - LAG) % U
                    dve.wait_ge(out_mm, t + 1)
                    dve.wait_ge(biased, t + 1)
                    dve.tensor_tensor(row[ut][:, :], o_ps[:, :], row[ut][:, :], ALU.add).then_inc(out_add, 1)
                if has(last):
                    for h in range(2):
                        dve.wait_ge(x2_h, 2 * last + 1 + h)
                        low(x2_lo[:, 4 * h:4 * h + 4, :].rearrange("p k r -> p (k r)"),
                            x_ps[:, h * 512:(h + 1) * 512],
                            x2_hi[:, 4 * h:4 * h + 4, :].rearrange("p k r -> p (k r)")).then_inc(x2_l, 1)

            dve.wait_ge(st_out, 3)
            low(bs_lo[:, :].rearrange("q (p j) -> q j p", j=KC), o_ps[:, :].rearrange("q (j p) -> q j p", j=KC),
                bs_hi[:, :].rearrange("q (p j) -> q j p", j=KC)).then_inc(bs_l, 1)
            for m in range(3):
                w_low(m)
            dve.wait_ge(back_h, 1)
            low(back_lo[:, :, :].rearrange("p a c -> p (a c)"), y[:, :],
                back_hi[:, 0:4, :].rearrange("p a c -> p (a c)")).then_inc(back_l, 1)
            w_low(3)
            spectrum_low(0)
            w_low(4)
            bx_masked(0)
            stack_low(0)
            w_low(5)
            slots(dve, slot)

        @blk.gpsimd
        def _(pool):
            regs = [pool.alloc_register(f"pool_wait{n}") for n in range(3)]
            for u in range(U):
                pool.memset(mix[u][:, :], 0.0)
            pool.memset(eo[:, 4, :], 0.0).then_inc(cleared, 1)

            def folds(g):
                pool.wait_ge(at_out, 2 * g + 2)
                fwd, rev = at[:, 1:H], at[:, L - 1:H:-1]
                pool.tensor_tensor(fold1[:, 0, 1:H], fwd, rev, ALU.add).then_inc(f1, 1)
                pool.tensor_tensor(fold1[:, 1, 1:H], fwd, rev, ALU.subtract).then_inc(f1, 1)
                pool.tensor_copy(fold1[:, 0, 0:H + 1:H], at[:, 0:H + 1:H]).then_inc(f1, 1)
                wait_apart(pool, regs, holds, (f1, 3 * g + 3), *([(bt_ps, g)] if from_first(g) else []))
                s, d = fold1[:, 0, :], fold1[:, 1, :]
                pool.tensor_tensor(fold2[:, 0, :], s[:, 0:Q], s[:, H:Q:-1], ALU.add).then_inc(f2, 1)
                pool.tensor_tensor(fold2[:, 1, :], s[:, 0:Q], s[:, H:Q:-1], ALU.subtract).then_inc(f2, 1)
                pool.tensor_tensor(fold2[:, 2, 1:Q], d[:, 1:Q], d[:, H - 1:Q:-1], ALU.subtract).then_inc(f2, 1)
                pool.tensor_tensor(fold2[:, 3, 1:Q], d[:, 1:Q], d[:, H - 1:Q:-1], ALU.add).then_inc(f2, 1)
                pool.tensor_copy(fold2[:, 2:4, 0:1], fold1[:, :, Q:Q + 1]).then_inc(f2, 1)

            def a_low(g):
                pool.wait_ge(g_h, 2 * g + 1)
                pool.tensor_tensor(g_lo[:, 0, :], at[:, :], g_hi[:, 0, :].bitcast(F32), ALU.subtract
                                   ).then_inc(g_lo_at, 1)

            def bias_added(t, u):
                pool.wait_ge(x2_mm, 2 * t + 2)
                pool.tensor_tensor(row[u][:, :], row[u][:, :], bias[:, :], ALU.add).then_inc(biased, 1)

            def gather(s, u):
                wait_apart(pool, regs, holds, (top_step, TOPS * s + 5), (y_saved, 32 * (s + 1)),
                           *([(sum_step, SUMS * s)] if from_first(s) else []))
                for n in range(NSEL):
                    if n >= RB:
                        wait_apart(pool, regs, holds, (top_step, TOPS * s + 11),
                                   (sum_step, SUMS * s + n - RB + 2))
                    pool.indirect_dma_start(out=rolled[n % RB][:, :], out_offset=None, in_=y2_d[u],
                                            in_offset=bass.IndirectOffsetOnAxis(ap=off[:, n:n + 1], axis=0)
                                            ).then_inc(rolled_in[n % RB], 16)

            def powers(s):
                n = [FS * s]

                def step(ins, wait=True):
                    ins.then_inc(fold_step, 1)
                    n[0] = n[0] + 1
                    if wait:
                        pool.wait_ge(fold_step, n[0])

                pool.wait_ge(sq_out, s + 1)
                if from_first(s):
                    pool.wait_ge(eo_h, s)
                    pool.wait_ge(eo_l, s)
                step(pool.tensor_tensor(eo[0:1, 4, :], sq[0:1, 0, 1, 0, :], sq[0:1, 0, 1, 1, :], ALU.add), False)
                wait_apart(pool, regs, holds, (fold_step, n[0]))
                step(pool.memset(sq[0:1, 0, 1, :, :], 0.0))
                for a in range(2):
                    step(pool.tensor_tensor(pw[a], pw[a], sq[:, a, 1, :, :].rearrange("p h r -> p (h r)"),
                                            ALU.add), a == 1)
                both = turn[:, :].rearrange("p (a b c) -> p a b c", a=2, b=2)[:, :, 0, :]
                step(pool.tensor_tensor(eo[:, 0:2, :], both[:, :, 0:P], both[:, :, P:2 * P], ALU.add), False)
                step(pool.tensor_tensor(eo[:, 2:4, :], both[:, :, 0:P], both[:, :, P:2 * P], ALU.subtract), False)

            def slot(s, u, i):
                t, last, g = s - LAG, s - 1, i + 1
                if has(t):
                    bias_added(t, (u - LAG) % U)
                if has(last):
                    gather(last, (u - 1) % U)
                if has_attn(s):
                    powers(s)
                if u == 0 and has_group(g):
                    folds(g)
                if u == 2 and has_group(g):
                    a_low(g)

            folds(0)
            a_low(0)
            pool.wait_ge(bias_in, 16)
            slots(pool, slot)


_INS = ["x", "itok_B_4_50", "itok_B_0_15", "L0_cond_A", "L0_cond_B", "L0_cond2_weights", "L0_ffn_W_base",
        "L0_ffn_b_base", "L0_ffn_W_router", "L0_ffn_A_stack", "L0_ffn_B_stack"]


def kernel(**inputs):
    import concourse.bacc as bacc
    from concourse.bass_utils import run_bass_kernel_spmd as run

    nc = bacc.Bacc("TRN2", target_bir_lowering=False, num_devices=1)
    arrays = {f"in_{name}": np.ascontiguousarray(inputs[name]) for name in _INS}
    arrays.update({f"const_{name}": a for name, a in constants().items()})
    args = [nc.dram_tensor(name, a.shape, mybir.dt.from_np(a.dtype), kind="ExternalInput").ap()
            for name, a in arrays.items()]
    args.append(nc.dram_tensor("out", (NS, C, L), F32, kind="ExternalOutput").ap())
    build(nc, *args)
    return run(nc, [arrays], core_ids=[0]).results[0]["out"]
```
